# Optimizing a Trainium2 kernel written in Bass

```python
import numpy as np
import jax
import jax.numpy as jnp

def _softmax(x, axis=-1):
    return jax.nn.softmax(x, axis=axis)

def _gelu(x):
    return jax.nn.gelu(x, approximate=True)

def _silu(x):
    return jax.nn.silu(x)

def _sigmoid(x):
    return jax.nn.sigmoid(x)

def _layernorm(x, axis=-1, eps=1e-05):
    m = jnp.mean(x, axis=axis, keepdims=True)
    v = jnp.var(x, axis=axis, keepdims=True)
    return (x - m) / jnp.sqrt(v + eps)

def _scatter_add(tgt, idx, src, axis=0):
    return tgt.at[idx].add(src)

def _segment_sum(src, seg, n):
    return jax.ops.segment_sum(src, seg, n)
kernel_name = 'mk_gnn_preln_d1_gnn_r64_1d5726'

def setup_inputs(seed: int=0):
    np.random.seed(seed)
    _w = jnp.asarray

    def _rec_inputs():
        import jax
        import jax.numpy as jnp
        _gk = jax.random.key(seed)
        x = -0.000202 + 1 * jax.random.normal(jax.random.fold_in(_gk, 1), (50000, 128), jnp.float32)
        src = jax.random.randint(jax.random.fold_in(_gk, 2), (25000,), 0, 50000, jnp.int32)
        dst = jax.random.randint(jax.random.fold_in(_gk, 3), (25000,), 0, 50000, jnp.int32)
        _o = jnp.argsort(dst, stable=True)
        src = src[_o]
        dst = dst[_o]
        edge_attr_42 = 0.000171677 + 1.0001 * jax.random.normal(jax.random.fold_in(_gk, 11), (25000, 42), jnp.float32)
        edge_weight = jax.random.uniform(jax.random.fold_in(_gk, 13), (25000,), jnp.float32, 0.0, 0.999998)
        node_vec = jax.random.uniform(jax.random.fold_in(_gk, 14), (50000,), jnp.float32, 0.0, 0.999994)
        return (x, src, dst, edge_attr_42, edge_weight, node_vec)
    x, src, dst, edge_attr_42, edge_weight, node_vec = _rec_inputs()

    def _L0_gnn_setup():
        import jax, jax.numpy as jnp
        import numpy as np
        NODE_EMB_DIM = 16
        NUM_REL = 10

        def _rgcn_layer(x, src, dst, edge_type, w_rel, root, bias):
            N = x.shape[0]
            seg = dst * NUM_REL + edge_type
            xs = x[src]
            sums = jax.ops.segment_sum(xs, seg, num_segments=N * NUM_REL)
            cnt = jax.ops.segment_sum(jnp.ones(seg.shape, x.dtype), seg, num_segments=N * NUM_REL)
            mean = (sums / jnp.maximum(cnt, 1.0)[:, None]).reshape(N, NUM_REL, -1)
            return jnp.einsum('nrd,rdo->no', mean, w_rel) + x @ root + bias
        key = jax.random.key(seed)
        ks = jax.random.split(key, 10)
        N, E, C = (50000, 12500, 128)
        s = 1.0 / np.sqrt(C).astype(np.float32)
        x = jax.random.normal(ks[0], (N, C), jnp.float32)
        last_update = jax.random.uniform(ks[1], (N,), jnp.float32)
        t = jax.random.uniform(ks[2], (E,), jnp.float32)
        msg = jax.random.normal(ks[3], (E, 2 * NODE_EMB_DIM + NUM_REL), jnp.float32)
        w_rel1 = jax.random.normal(ks[4], (NUM_REL, C, C), jnp.float32) * s
        root1 = jax.random.normal(ks[5], (C, C), jnp.float32) * s
        b1 = jnp.zeros((C,), jnp.float32)
        w_rel2 = jax.random.normal(ks[6], (NUM_REL, C, C), jnp.float32) * s
        root2 = jax.random.normal(ks[7], (C, C), jnp.float32) * s
        b2 = jnp.zeros((C,), jnp.float32)
        edge_index = jax.random.randint(ks[8], (2, E), 0, N, dtype=jnp.int32)
        return dict(x=x, last_update=last_update, t=t, msg=msg, w_rel1=w_rel1, root1=root1, b1=b1, w_rel2=w_rel2, root2=root2, b2=b2, edge_index=edge_index)
    _L0_gnn_all = _L0_gnn_setup()
    _L0_gnn_in = {k: v for k, v in _L0_gnn_all.items() if k in ('w_rel1', 'root1', 'b1', 'w_rel2', 'root2', 'b2')}
    del _L0_gnn_all
    return {'x': x, 'src': src, 'dst': dst, 'edge_attr_42': edge_attr_42, 'edge_weight': edge_weight, 'node_vec': node_vec, 'L0_gnn_w_rel1': _L0_gnn_in['w_rel1'], 'L0_gnn_root1': _L0_gnn_in['root1'], 'L0_gnn_b1': _L0_gnn_in['b1'], 'L0_gnn_w_rel2': _L0_gnn_in['w_rel2'], 'L0_gnn_root2': _L0_gnn_in['root2'], 'L0_gnn_b2': _L0_gnn_in['b2']}

def reference(x, src, dst, edge_attr_42, edge_weight, node_vec, L0_gnn_w_rel1, L0_gnn_root1, L0_gnn_b1, L0_gnn_w_rel2, L0_gnn_root2, L0_gnn_b2):
    import jax
    import jax.numpy as jnp

    def _L0_gnn_ref(x, last_update, t, msg, w_rel1, root1, b1, w_rel2, root2, b2, edge_index):
        import jax, jax.numpy as jnp
        import numpy as np
        NODE_EMB_DIM = 16
        NUM_REL = 10

        def _rgcn_layer(x, src, dst, edge_type, w_rel, root, bias):
            N = x.shape[0]
            seg = dst * NUM_REL + edge_type
            xs = x[src]
            sums = jax.ops.segment_sum(xs, seg, num_segments=N * NUM_REL)
            cnt = jax.ops.segment_sum(jnp.ones(seg.shape, x.dtype), seg, num_segments=N * NUM_REL)
            mean = (sums / jnp.maximum(cnt, 1.0)[:, None]).reshape(N, NUM_REL, -1)
            return jnp.einsum('nrd,rdo->no', mean, w_rel) + x @ root + bias
        src, dst = (edge_index[0], edge_index[1])
        edge_type = jnp.argmax(msg[:, NODE_EMB_DIM:-NODE_EMB_DIM], axis=1).astype(jnp.int32)
        h = jax.nn.relu(_rgcn_layer(x, src, dst, edge_type, w_rel1, root1, b1))
        return _rgcn_layer(h, src, dst, edge_type, w_rel2, root2, b2)
    edge_index = jnp.stack([src, dst])
    h = jnp.maximum(_layernorm(x, axis=-1), 0.0)
    x = x + _L0_gnn_ref(h, node_vec, edge_weight, edge_attr_42, L0_gnn_w_rel1, L0_gnn_root1, L0_gnn_b1, L0_gnn_w_rel2, L0_gnn_root2, L0_gnn_b2, edge_index)
    return x

_drawn_inputs = setup_inputs


def setup_inputs(seed=0):
    import zlib

    import numpy as np

    out = dict(_drawn_inputs(seed))
    spreads = {'L0_gnn_b1': (0.0, 0.1), 'L0_gnn_b2': (0.0, 0.1)}
    factors = {}
    for name, (base, spread) in spreads.items():
        noise = np.random.default_rng([zlib.crc32(name.encode()), seed]).standard_normal(out[name].shape)
        drawn = base * np.exp(spread * noise) if base else spread * noise
        out[name] = jnp.asarray(drawn.astype(out[name].dtype))
    for name, factor in factors.items():
        out[name] = (out[name] * factor).astype(out[name].dtype)
    return out
```

```python
import concourse.bass as bass
from concourse import mybir
from contextlib import ExitStack

F32, I32, BF16 = mybir.dt.float32, mybir.dt.int32, mybir.dt.bfloat16
ALU, ACT, AX = mybir.AluOpType, mybir.ActivationFunctionType, mybir.AxisListType

P = 128
N, C, E, R = 50000, 128, 25000, 10
ATTR, REL0 = 42, 16
EPS = 1e-5
K = 8
HT = K // 2
HC = HT * C
GROUP = K * P
J = -(-E // P)
TAIL_P, TAIL_J = E // J, E % J
NG = -(-N // GROUP)
TILES = -(-((E + R * (P - 1)) // P) // K) * K
EG = TILES // K
SLOTS = TILES * P
HR = TILES // 2
SPARE = 2 * GROUP
KEY = 1 << 16
PADKEY = R * KEY
TROWS = -(-(SLOTS + 2) // P) * P
SKIP = 1 << 20
SCAT = 14
assert J % (2 * SCAT) == 0 and NG % 2 == 1 and EG % 2 == 0 and 2 * (EG - 2) == NG - 1 and HR <= P


def wait(eng, sem, value):
    if not (isinstance(value, int) and value <= 0):
        eng.wait_ge(sem, value)


def alone(eng, ticks):
    eng.sem_inc(ticks, 1)


class Own:

    def __init__(self, eng, sem):
        self.eng, self.sem, self.base, self.n = eng, sem, 0, 0

    def done(self, ins):
        ins.then_inc(self.sem, 1)
        self.n += 1
        self.eng.wait_ge(self.sem, self.base + self.n)

    def enter(self, i, per):
        self.start = self.base + self.n if self.n or isinstance(self.base, int) else self.start
        self.base, self.per, self.n = self.start + i * per, per, 0

    def leave(self, times):
        assert self.n == self.per, (self.n, self.per)
        self.base, self.n = self.start + times * self.per, 0


def build(nc, x, src, dst, attr, w_rel1, root1, b1, w_rel2, root2, b2, out):
    ctx = ExitStack()
    with ctx:
        def sb(name, shape, dt=F32):
            return ctx.enter_context(nc.sbuf_tensor(name, shape, dt))

        def sem(name):
            return ctx.enter_context(nc.semaphore(name))

        def dram(name, shape, dt=F32):
            return nc.dram_tensor(name, shape, dt, kind="Internal").ap()

        pre1 = dram("pre1", (N + SPARE, C))
        table = dram("slot_table", (TROWS, 2))
        mask_d = dram("mask_d", (TILES, P), BF16)

        w1, w2 = sb("w1", [P, R * C]), sb("w2", [P, R * C])
        r1, r2 = sb("r1", [P, C]), sb("r2", [P, C])
        b1b, b2b = sb("b1b", [P, C]), sb("b2b", [P, C])
        ident, tri, ones = sb("ident", [P, P]), sb("tri", [P, P]), sb("ones", [P, P])
        eps = sb("eps", [P, 1])

        msg2 = sb("msg2", [P, TILES, C])
        scratch = msg2[:, :, :].rearrange("p t c -> p (t c)")
        at = [0]

        def carve(n, dt=F32):
            at[0] += n
            assert at[0] <= TILES * C
            v = scratch[:, at[0] - n:at[0]]
            return v if dt is F32 else v.bitcast(dt)

        attr_s = carve(J * ATTR).rearrange("p (j a) -> p j a", a=ATTR)
        cand = carve(J * R).rearrange("p (j r) -> p j r", r=R)
        hot = carve(R * J).rearrange("p (r j) -> p r j", r=R)
        goes_on = carve(R * J).rearrange("p (r j) -> p r j", r=R)
        rank = carve(R * J).rearrange("p (r j) -> p r j", r=R)
        src_i0, dst_i0 = carve(J, I32), carve(J, I32)
        e_no, best, rel, void = carve(J), carve(J), carve(J), carve(J)
        row_f, row_i = carve(J), carve(J, I32)
        rec = carve(J * 2).rearrange("p (j c) -> p j c", c=2)
        r_no = carve(R)
        both = carve(2 * R)
        n_i, n_f, n_sum, shift = carve(R, I32), carve(R), carve(R), carve(R)
        fill = carve(TROWS // P * 2).rearrange("p (j c) -> p j c", c=2)
        zeros = carve(SPARE // P * C)
        cur = carve(2 * P * 2).rearrange("p (h i c) -> p h i c", h=2, c=2)
        prev = carve(2 * P * 2).rearrange("p (h i c) -> p h i c", h=2, c=2)
        nxt = carve(2 * P * 2).rearrange("p (h i c) -> p h i c", h=2, c=2)

        def halves(dt=F32):
            return carve(2 * P, dt).rearrange("p (h i) -> p h i", h=2)

        s_no, same, last, first, begun, count, recip, node, spare, aim = (halves() for _ in range(10))
        s_i, key_i, node_i = halves(I32), halves(I32), halves(I32)
        carry = carve(2)
        rel_ri, rel_rf = carve(2, I32), carve(2)
        tops, top_sum = carve(TILES + 1), carve(TILES + 1)
        rel_c, power, flag = carve(TILES), carve(TILES), carve(TILES)
        flag_f = carve(EG)

        same_b = sb("same_b", [P, 2, P], BF16)
        src_all, aim_all = sb("src_all", [P, TILES], I32), sb("aim_all", [P, TILES], I32)
        rc_all = sb("rc_all", [P, TILES])
        wcol = sb("wcol", [1, TILES], I32)
        starts = sb("starts", [1, EG], I32)

        stage_i = sb("stage_i", [P, 2, SCAT], I32)
        stage_r = sb("stage_r", [P, 2, SCAT, 2])
        g_idx, s_idx = sb("g_idx", [P, 2, K], I32), sb("s_idx", [P, 2, K], I32)
        eg, eh = sb("eg", [P, 2, K, C]), sb("eh", [P, 2, K, C])
        sums = sb("sums", [P, 2, GROUP])
        mask = sb("mask", [P, 2, GROUP], BF16)
        msg = sb("msg", [P, 2, K, C])
        dx = sb("dx", [P, 2, K, C])
        dh = sb("dh", [P, 2, K, C])
        dT = sb("dT", [P, 2, GROUP])
        do = sb("do", [P, 2, K, C])
        d_st, e_st = sb("d_st", [P, K, 6]), sb("e_st", [P, K, 6])
        d_mv, e_mv = sb("d_mv", [P, 2, K, 2]), sb("e_mv", [P, 2, K, 2])
        d_neg, d_sd, d_rs = sb("d_neg", [P, 2, K]), sb("d_sd", [P, 2, K]), sb("d_rs", [P, 2, K])
        e_neg, e_sd, e_rs = sb("e_neg", [P, 2, K]), sb("e_sd", [P, 2, K]), sb("e_rs", [P, 2, K])

        ps = [ctx.enter_context(nc.psum_tensor(f"bank{n}", [P, HC], F32)) for n in range(8)]
        Td, Te, Md, Me = ps[0:2], ps[2:4], ps[4:6], ps[6:8]

        S = {}
        for name in ("attr_in ids_in consts_in made pads_set filled spare_zero rec_ready offs sorted "
                     "m_in tops_t tops_in tops_b metaT mask_out meta gidx_set "
                     "d1_mean d1_std d1_relu d1_T d1_hT d1_M d1_evac "
                     "e1_mean e1_std e1_par e1_relu e1_T e1_scan e1_M e1_evac "
                     "d2_T d2_hT d2_M d2_evac e2_relu e2_T e2_scan e2_M e2_evac staged "
                     "dve_own pool_own dve_ticks pool_ticks").split():
            S[name] = sem(name)
        for name in "rec_out d1_in d1_stored e1_in mask_in e1_add d2_in d2_stored e2_in mask2_in e2_add".split():
            S[name] = [sem(f"{name}{n}") for n in range(2)]

        block = ctx.enter_context(nc.Block())

        def rows(a, g):
            base = g * GROUP if not isinstance(g, int) else min(g * GROUP, N - GROUP)
            return a[bass.ds(base, GROUP), :].rearrange("(p k) c -> p (k c)", k=K)

        def flat(t, par):
            return t[:, par, :, :].rearrange("p k c -> p (k c)")

        def shifted(by):
            return [table[by + h * HR * P:by + (h + 1) * HR * P, :].rearrange("(t i) c -> t (i c)", i=P)
                    for h in range(2)]

        @block.sync
        def _(sp):
            whole = TAIL_P // 16 * 16
            sp.wait_ge(S["pads_set"], 1)
            for a, t, w, done in ((attr, attr_s.rearrange("p j a -> p (j a)"), ATTR, "attr_in"),
                                  (src, src_i0, 1, "ids_in"), (dst, dst_i0, 1, "ids_in")):
                v = a[0:TAIL_P * J].rearrange("(p j) a -> p (j a)", j=J)
                sp.dma_start(t[0:whole, :], v[0:whole, :]).then_inc(S[done], 16)
                sp.dma_start(t[whole:TAIL_P, :], v[whole:TAIL_P, :]).then_inc(S[done], 16)
                tail = a[TAIL_P * J:E].rearrange("(p j) a -> p (j a)", p=1)
                sp.dma_start(t[TAIL_P:TAIL_P + 1, 0:TAIL_J * w], tail).then_inc(S[done], 16)
            sp.dma_start(table.rearrange("(p j) c -> p (j c)", p=P),
                         fill.rearrange("p j c -> p (j c)")).then_inc(S["filled"], 16)
            for t in (pre1, out):
                sp.dma_start(t[N:N + SPARE, :].rearrange("(p k) c -> p (k c)", p=P),
                             zeros).then_inc(S["spare_zero"], 16)
            for t, a in ((w1, w_rel1), (w2, w_rel2)):
                sp.dma_start(t[:, :].rearrange("c (r o) -> c r o", r=R),
                             a.rearrange("r c o -> c r o")).then_inc(S["consts_in"], 16)
            for t, a in ((r1, root1), (r2, root2), (b1b, b1.partition_broadcast(P)),
                         (b2b, b2.partition_broadcast(P))):
                sp.dma_start(t[:, :], a).then_inc(S["consts_in"], 16)

            def load1(g, i, par):
                wait(sp, S["d1_relu"], 2 * g - 2)
                sp.dma_start(flat(dx, par), rows(x, g)).then_inc(S["d1_in"][par], 16)

            def store1(g, par):
                sp.wait_ge(S["d1_evac"], 2 * g + 2)
                sp.dma_start(rows(pre1, g), flat(do, par)).then_inc(S["d1_stored"][par], 16)

            def pair1(i):
                load1(2 * i + 2, i, 0)
                store1(2 * i, 0)
                load1(2 * i + 3, i, 1)
                store1(2 * i + 1, 1)

            load1(0, 0, 0)
            load1(1, 0, 1)
            pair1(0)
            with sp.Fori(1, NG // 2 - 1) as i:
                pair1(i)
            load1(NG - 1, 0, 0)
            store1(NG - 3, 0)
            store1(NG - 2, 1)
            sp.wait_ge(S["d1_stored"][1], 16 * (NG // 2))
            store1(NG - 1, 0)

            for par in range(2):
                sp.wait_ge(S["rec_out"][par], 16 * J // 2)
            for t, by in ((cur, 1), (prev, 0), (nxt, 2)):
                for h, v in enumerate(shifted(by)):
                    sp.dma_start(t[0:HR, h].rearrange("p i c -> p (i c)"), v).then_inc(S["m_in"], 16)
            sp.wait_ge(S["meta"], 1)
            for h in range(2):
                sp.dma_start(mask_d[h * HR:(h + 1) * HR, :], same_b[0:HR, h, :]).then_inc(S["mask_out"], 16)
            sp.wait_ge(S["mask_out"], 32)

            def load_mask(e, par, scan, done):
                wait(sp, S[scan], 2 * e - 2)
                v = mask_d[bass.ds(e * K, K), :].rearrange("t i -> (t i)").partition_broadcast(P)
                sp.dma_start(mask[:, par, :], v).then_inc(S[done][par], 16)

            def masks1(i):
                for par in range(2):
                    load_mask(2 * i + par, par, "e1_scan", "mask_in")

            masks1(0)
            with sp.Fori(1, EG // 2) as i:
                masks1(i)

            for par in range(2):
                sp.wait_ge(S["e1_add"][par], 16 * K * EG // 2)

            def load2(g, par):
                wait(sp, S["d2_T"], 2 * g - 2)
                sp.dma_start(flat(dh, par), rows(pre1, g)).then_inc(S["d2_in"][par], 16)
                wait(sp, S["d2_evac"], 2 * g - 2)
                sp.dma_start(flat(dx, par), rows(x, g)).then_inc(S["d2_in"][par], 16)

            def store2(g, par):
                sp.wait_ge(S["d2_evac"], 2 * g + 2)
                sp.dma_start(rows(out, g), flat(do, par)).then_inc(S["d2_stored"][par], 16)

            def step2(j, epar, more):
                load_mask(j, epar, "e2_scan", "mask2_in")
                store2(2 * j, 0)
                load2(2 * j + 2, 0)
                store2(2 * j + 1, 1)
                if more:
                    load2(2 * j + 3, 1)

            load2(0, 0)
            load2(1, 1)
            step2(0, 0, True)
            step2(1, 1, True)
            with sp.Fori(1, (EG - 2) // 2 - 1) as i:
                step2(2 * i, 0, True)
                step2(2 * i + 1, 1, True)
            step2(EG - 4, 0, True)
            step2(EG - 3, 1, False)
            load_mask(EG - 2, 0, "e2_scan", "mask2_in")
            load_mask(EG - 1, 1, "e2_scan", "mask2_in")
            sp.wait_ge(S["d2_stored"][1], 16 * (NG // 2))
            store2(NG - 1, 0)
            sp.wait_ge(S["d2_stored"][0], 16 * (NG // 2 + 1))

        @block.gpsimd
        def _(pool):
            own = Own(pool, S["pool_own"])
            pool.memset(ident[:, :], 0.0)
            own.done(pool.memset(ones[:, :], 1.0))
            pool.affine_select(out=ident[:, :], in_=ident[:, :], compare_op=ALU.not_equal, fill=1.0,
                               base=0, pattern=[[-1, P]], channel_multiplier=1)
            pool.affine_select(out=tri[:, :], in_=ones[:, :], compare_op=ALU.is_gt, fill=0.0,
                               base=0, pattern=[[1, P]], channel_multiplier=-1)
            pool.iota(e_no, pattern=[[1, J]], base=0, channel_multiplier=J,
                      allow_small_or_imprecise_dtypes=True)
            pool.iota(r_no, pattern=[[1, R]], base=0, channel_multiplier=0,
                      allow_small_or_imprecise_dtypes=True)
            pool.iota(s_no[0:HR], pattern=[[HR * P, 2], [1, P]], base=0, channel_multiplier=P,
                      allow_small_or_imprecise_dtypes=True)
            pool.iota(s_i[0:HR], pattern=[[HR * P, 2], [1, P]], base=0,
                      channel_multiplier=P).then_inc(S["made"], 1)

            pool.wait_ge(S["filled"], 16)
            pool.wait_ge(S["sorted"], 1)

            def scatter_records(i):
                for par in range(2):
                    j0 = (2 * i + par) * SCAT
                    wait(pool, S["rec_out"][par], 16 * SCAT * i)
                    pool.tensor_copy(stage_i[:, par, :], row_i[:, bass.ds(j0, SCAT)])
                    own.done(pool.tensor_copy(stage_r[:, par, :, :], rec[:, bass.ds(j0, SCAT), :]))
                    alone(pool, S["pool_ticks"])
                    for k in range(SCAT):
                        pool.indirect_dma_start(
                            table, bass.IndirectOffsetOnAxis(ap=stage_i[:, par, k:k + 1], axis=0),
                            stage_r[:, par, k, :], None, bounds_check=TROWS - 1,
                            oob_is_err=False).then_inc(S["rec_out"][par], 16)

            scatter_records(0)
            with pool.Fori(1, J // (2 * SCAT)) as i:
                own.enter(i - 1, 2)
                scatter_records(i)
            own.leave(J // (2 * SCAT) - 1)

            def gather(table_, e, i, par, free, done):
                wait(pool, S[free], (2 if free == "e1_relu" else 1) * (e - 1))
                own.done(pool.tensor_copy(g_idx[:, par, :], src_all[:, bass.ds(e * K, K)]))
                alone(pool, S["pool_ticks"])
                for k in range(K):
                    pool.indirect_dma_start(
                        eg[:, par, k, :], None, table_,
                        bass.IndirectOffsetOnAxis(ap=g_idx[:, par, k:k + 1], axis=0)
                    ).then_inc(S[done][par], 16)

            def scatter_add(table_, e, i, par, done):
                wait(pool, S[done][par], 16 * K * i)
                own.done(pool.tensor_copy(s_idx[:, par, :], aim_all[:, bass.ds(e * K, K)]))
                alone(pool, S["pool_ticks"])
                bits = pool.value_load(starts[0:1, bass.ds(e, 1)], min_val=0, max_val=(1 << K) - 1)

                def add(k):
                    pool.indirect_dma_start(
                        table_, bass.IndirectOffsetOnAxis(ap=s_idx[:, par, k:k + 1], axis=0),
                        msg[:, par, k, :], None, compute_op=ALU.add).then_inc(S[done][par], 16)

                def all_earlier(k):
                    wait(pool, S[done][par], 16 * (K * i + k))
                    wait(pool, S[done][1 - par], 16 * K * (i + par))
                    alone(pool, S["pool_ticks"])

                with pool.If(bits):
                    for k in range(K):
                        all_earlier(k)
                        add(k)
                with pool.Else():
                    for k in range(K):
                        add(k)

            pool.wait_ge(S["meta"], 2)

            def pair1(i, more=True):
                for par in range(2):
                    if more or par == 0:
                        gather(x, 2 * i + par + 1, i, 1 - par, "e1_relu", "e1_in")
                    if isinstance(i, int) and i == 0 and par == 0:
                        pool.wait_ge(S["spare_zero"], 32)
                        pool.wait_ge(S["d1_stored"][0], 16 * (NG // 2 + 1))
                        pool.wait_ge(S["d1_stored"][1], 16 * (NG // 2))
                    pool.wait_ge(S["e1_evac"], 2 * (2 * i + par) + 2)
                    scatter_add(pre1, 2 * i + par, i, par, "e1_add")

            gather(x, 0, 0, 0, "e1_relu", "e1_in")
            pair1(0)
            with pool.Fori(1, EG // 2 - 1) as i:
                own.enter(i - 1, 4)
                pair1(i)
            own.leave(EG // 2 - 2)
            pair1(EG // 2 - 1, more=False)

            for par in range(2):
                pool.wait_ge(S["e1_add"][par], 16 * K * EG // 2)

            def gathers2(i):
                for par in range(2):
                    gather(pre1, 2 * i + par, i, par, "e2_relu", "e2_in")

            gathers2(0)
            with pool.Fori(1, EG // 2) as i:
                own.enter(i - 1, 2)
                gathers2(i)
            own.leave(EG // 2 - 1)

            pool.wait_ge(S["d2_stored"][0], 16 * (NG // 2 + 1))
            pool.wait_ge(S["d2_stored"][1], 16 * (NG // 2))

            def adds2(i):
                for par in range(2):
                    pool.wait_ge(S["staged"], 2 * i + par + 1)
                    scatter_add(out, 2 * i + par, i, par, "e2_add")

            adds2(0)
            with pool.Fori(1, EG // 2) as i:
                own.enter(i - 1, 2)
                adds2(i)
            own.leave(EG // 2 - 1)
            for par in range(2):
                pool.wait_ge(S["e2_add"][par], 16 * K * EG // 2)

        @block.vector
        def _(dve):
            own = Own(dve, S["dve_own"])
            V = nc.vector
            q = TAIL_P // 32 * 32
            V.memset(attr_s[q:P, TAIL_J:J, REL0:REL0 + R], 0.0)
            V.memset(src_i0[q:P, TAIL_J:J], 0)
            V.memset(dst_i0[q:P, TAIL_J:J], 0)
            V.memset(zeros, 0.0)
            V.memset(fill[:, :, 0], 0.0)
            V.memset(eps[:, :], EPS)
            V.memset(fill[:, :, 1], float(PADKEY)).then_inc(S["pads_set"], 1)
            own.done(V.memset(goes_on, 1.0))
            own.done(V.memset(goes_on[:, :, 0], 0.0))

            dve.wait_ge(S["made"], 1)
            dve.wait_ge(S["attr_in"], 48)
            scores = attr_s[:, :, REL0:REL0 + R]
            own.done(V.tensor_reduce(best, scores, axis=AX.X, op=ALU.max))
            own.done(V.tensor_tensor(cand, scores, best.unsqueeze(2).to_broadcast([P, J, R]), ALU.is_equal))
            own.done(V.scalar_tensor_tensor(cand, cand, -float(R), r_no.unsqueeze(1).to_broadcast([P, J, R]),
                                            ALU.mult, ALU.add))
            own.done(V.tensor_reduce(rel, cand, axis=AX.X, op=ALU.min))
            V.tensor_scalar(rel, rel, float(R), None, ALU.add)
            own.done(V.tensor_scalar(void, e_no, float(E), None, ALU.is_ge))
            own.done(V.scalar_tensor_tensor(rel, void, float(2 * R), rel, ALU.mult, ALU.add))
            own.done(V.tensor_tensor(hot, rel.unsqueeze(1).to_broadcast([P, R, J]),
                                     r_no.unsqueeze(2).to_broadcast([P, R, J]), ALU.is_equal))
            own.done(V.tensor_tensor_scan(rank.rearrange("p r j -> p (r j)"),
                                          goes_on.rearrange("p r j -> p (r j)"),
                                          hot.rearrange("p r j -> p (r j)"), 0.0, ALU.mult, ALU.add))
            V.tensor_copy(n_f, rank[:, :, J - 1]).then_inc(S["rec_ready"], 1)
            dve.wait_ge(S["ids_in"], 96)
            V.tensor_copy(rec[:, :, 0], src_i0)
            own.done(V.tensor_copy(row_f, dst_i0))
            own.done(V.scalar_tensor_tensor(rec[:, :, 1], rel, float(KEY), row_f, ALU.mult, ALU.add))
            dve.wait_ge(S["offs"], 1)
            own.done(V.tensor_copy(both, Me[0][:, 0:2 * R]))
            own.done(V.tensor_scalar(n_i, both[:, R:2 * R], float(P - 1), None, ALU.add))
            own.done(V.tensor_scalar(n_i, n_i, 7, None, ALU.logical_shift_right))
            own.done(V.tensor_copy(n_f, n_i))
            own.done(V.tensor_tensor_scan(n_sum, ones[:, 0:R], n_f, 0.0, ALU.mult, ALU.add))
            own.done(V.tensor_tensor(n_sum, n_sum, n_f, ALU.subtract))
            own.done(V.scalar_tensor_tensor(shift, n_sum, float(P), both[:, 0:R], ALU.mult, ALU.add))
            own.done(V.tensor_tensor(rank, rank, shift.unsqueeze(2).to_broadcast([P, R, J]), ALU.add))
            own.done(V.tensor_tensor(rank, rank, hot, ALU.mult))
            own.done(V.tensor_reduce(row_f, rank.rearrange("p r j -> p j r"), axis=AX.X, op=ALU.add))
            own.done(V.scalar_tensor_tensor(row_f, void, float(SKIP), row_f, ALU.mult, ALU.add))
            V.tensor_copy(row_i, row_f).then_inc(S["sorted"], 1)

            def stats(t, par, st, mv):
                for k in range(K):
                    ins = V.bn_stats(st[:, k, :], t[:, par, k, :])
                own.done(ins)
                alone(dve, S["dve_ticks"])
                for k in range(K):
                    ins = V.bn_aggr(mv[:, par, k, :], st[:, k, :])
                return ins

            def front1(g, i, par):
                dve.wait_ge(S["d1_in"][par], 16 * (i + 1))
                wait(dve, S["d1_relu"], 2 * g - 2)
                own.done(stats(dx, par, d_st, d_mv))
                V.tensor_scalar(d_neg[:, par, :], d_mv[:, par, :, 0], -1.0, None,
                                ALU.mult).then_inc(S["d1_mean"], 1)

            def back1(g, i, par):
                dve.wait_ge(S["d1_std"], g + 1)
                own.done(V.reciprocal(d_rs[:, par, :], d_sd[:, par, :]))
                wait(dve, S["d1_stored"][par], 16 * i)
                for h in range(2):
                    dve.wait_ge(S["d1_M"], 2 * g + h + 1)
                    for k in range(HT * h, HT * h + HT):
                        m = Md[h][:, (k - HT * h) * C:(k - HT * h + 1) * C]
                        ins = V.scalar_tensor_tensor(do[:, par, k, :], m, d_rs[:, par, k:k + 1], b1b[:, :],
                                                     ALU.mult, ALU.add)
                    ins.then_inc(S["d1_evac"], 1)

            def pair1(i, last=False):
                front1(2 * i + 1, i, 1)
                back1(2 * i, i, 0)
                front1(2 * i + 2, i + 1, 0)
                back1(2 * i + 1, i, 1)

            dve.wait_ge(S["consts_in"], 96)
            front1(0, 0, 0)
            pair1(0)
            with dve.Fori(1, NG // 2) as i:
                own.enter(i - 1, 6)
                pair1(i)
            own.leave(NG // 2 - 1)
            back1(NG - 1, NG // 2, 0)

            dve.wait_ge(S["m_in"], 96)
            key = cur[0:HR, :, :, 1]
            r = slice(0, HR)
            V.tensor_tensor(same[r], key, prev[r, :, :, 1], ALU.is_equal)
            V.tensor_tensor(last[r], key, nxt[r, :, :, 1], ALU.not_equal)
            V.tensor_copy(key_i[r], key)
            V.tensor_scalar(first[r], key, float(PADKEY), None, ALU.is_lt)
            own.done(V.tensor_scalar(node_i[r], s_i[r], SPARE - 1, None, ALU.bitwise_and))
            V.tensor_copy(same_b[r], same[r]).then_inc(S["meta"], 1)
            V.tensor_tensor(last[r], last[r], first[r], ALU.mult)
            V.tensor_copy(spare[r], node_i[r])
            own.done(V.tensor_scalar(rel_ri[r], key_i[r, :, 0], 16, None, ALU.logical_shift_right))
            V.tensor_scalar(node_i[r], key_i[r], KEY - 1, None, ALU.bitwise_and)
            V.tensor_scalar(spare[r], spare[r], float(N), None, ALU.add)
            V.tensor_copy(rel_rf[r], rel_ri[r])
            own.done(V.tensor_scalar(first[r], same[r], -1.0, 1.0, ALU.mult, ALU.add))
            V.tensor_scalar(rel_rf[r], rel_rf[r], float(R - 1), float(C), ALU.min, ALU.mult)
            V.tensor_copy(node[r], node_i[r])
            own.done(V.tensor_tensor(first[r], first[r], s_no[r], ALU.mult))
            for h in range(2):
                ins = V.tensor_tensor_scan(begun[r, h], first[r, h], first[r, h], 0.0, ALU.max, ALU.max)
            ins.then_inc(S["tops_in"], 1)
            own.done(V.tensor_tensor(node[r], node[r], spare[r], ALU.subtract))
            own.done(V.tensor_tensor(node[r], node[r], last[r], ALU.mult))
            own.done(V.tensor_tensor(aim[r], node[r], spare[r], ALU.add))
            V.memset(tops[0:1, 0:1], 0.0)
            dve.wait_ge(S["tops_t"], 1)
            V.tensor_copy(tops[0:1, 1:TILES + 1], Td[0][0:1, 0:TILES])
            own.done(V.tensor_copy(rel_c[0:1], Td[1][0:1, 0:TILES]))
            V.tensor_tensor_scan(top_sum[0:1], tops[0:1], tops[0:1], 0.0, ALU.max,
                                 ALU.max).then_inc(S["tops_in"], 1)
            V.tensor_copy(wcol[0:1, :], rel_c[0:1])
            for k in range(K):
                V.memset(power[0:1].rearrange("p (g k) -> p g k", k=K)[:, :, k], float(1 << k))
            V.memset(flag[0:1, 0:1], 0.0)
            own.done(V.tensor_tensor(flag[0:1, 1:TILES], rel_c[0:1, 1:TILES], rel_c[0:1, 0:TILES - 1],
                                     ALU.not_equal))
            own.done(V.tensor_tensor(flag[0:1], flag[0:1], power[0:1], ALU.mult))
            own.done(V.tensor_reduce(flag_f[0:1], flag[0:1].rearrange("p (g k) -> p g k", k=K),
                                     axis=AX.X, op=ALU.add))
            V.tensor_copy(starts[0:1, :], flag_f[0:1])
            dve.wait_ge(S["tops_b"], 1)
            own.done(V.tensor_copy(carry[r], Te[0][r, 0:2]))
            own.done(V.tensor_tensor(begun[r], begun[r], carry[r].unsqueeze(2).to_broadcast([HR, 2, P]), ALU.max))
            own.done(V.scalar_tensor_tensor(count[r], s_no[r], 1.0, begun[r], ALU.add, ALU.subtract))
            V.reciprocal(recip[r], count[r]).then_inc(S["tops_in"], 1)
            dve.wait_ge(S["metaT"], 1)
            V.tensor_copy(src_all[:, :], Td[0][:, 0:TILES])
            V.tensor_copy(aim_all[:, :], Td[1][:, 0:TILES])
            V.tensor_copy(rc_all[:, :], Te[1][:, 0:TILES]).then_inc(S["meta"], 1)

            def scan(e, i, par, L, mask_in):
                for h in range(2):
                    dve.wait_ge(S[L + "_T"], 2 * e + h + 1)
                    dve.wait_ge(S[mask_in][par], 16 * (i + 1))
                    wait(dve, S[L + "_M"], 2 * e + h - 3)
                    wait(dve, S[L + "_scan"], 2 * e + h)
                    before = sums[:, par, HC - 1:HC] if h else sums[:, 1 - par, GROUP - 1:GROUP]
                    if h == 0 and isinstance(e, int) and e == 0:
                        before = 0.0
                    V.tensor_tensor_scan(sums[:, par, h * HC:(h + 1) * HC], mask[:, par, h * HC:(h + 1) * HC],
                                         (Te[h])[:, :], before, ALU.mult, ALU.add).then_inc(S[L + "_scan"], 1)

            def over_count(e, h, to, L):
                dve.wait_ge(S[L + "_M"], 2 * e + h + 1)
                rc = rc_all[:, bass.ds(K * e + HT * h, HT)].unsqueeze(2).to_broadcast([P, HT, C])
                V.tensor_tensor(to, Me[h][:, :].rearrange("p (k c) -> p k c", c=C), rc,
                                ALU.mult).then_inc(S[L + "_evac"], 1)

            def edges1(i):
                for par in range(2):
                    e = 2 * i + par
                    dve.wait_ge(S["e1_in"][par], 16 * K * (i + 1))
                    wait(dve, S["e1_relu"], 2 * e - 2)
                    stats(eg, par, e_st, e_mv).then_inc(S["e1_mean"], 1)
                    dve.wait_ge(S["e1_std"], e + 1)
                    own.done(V.reciprocal(e_rs[:, par, :], e_sd[:, par, :]))
                    V.scalar_tensor_tensor(e_neg[:, par, :], e_mv[:, par, :, 0], -1.0, e_rs[:, par, :],
                                           ALU.mult, ALU.mult).then_inc(S["e1_par"], 1)
                    scan(e, i, par, "e1", "mask_in")
                    wait(dve, S["e1_add"][par], 16 * K * i)
                    for h in range(2):
                        over_count(e, h, msg[:, par, HT * h:HT * h + HT, :], "e1")

            edges1(0)
            with dve.Fori(1, EG // 2) as i:
                own.enter(i - 1, 4)
                edges1(i)
            own.leave(EG // 2 - 1)

            for par in range(2):
                dve.wait_ge(S["e1_add"][par], 16 * K * EG // 2)

            def residual(g, i, par):
                dve.wait_ge(S["d2_in"][par], 32 * (i + 1))
                wait(dve, S["d2_stored"][par], 16 * i)
                own.done(V.tensor_tensor(do[:, par, :, :], dx[:, par, :, :],
                                         b2b[:, :].unsqueeze(1).to_broadcast([P, K, C]), ALU.add))

            def back2(g, par):
                for h in range(2):
                    dve.wait_ge(S["d2_M"], 2 * g + h + 1)
                    o = flat(do, par)[:, h * HC:(h + 1) * HC]
                    V.tensor_tensor(o, Md[h][:, :], o, ALU.add).then_inc(S["d2_evac"], 1)

            def edge_out(e):
                for h in range(2):
                    over_count(e, h, msg2[:, bass.ds(K * e + HT * h, HT), :], "e2")

            def step2(j, i, epar):
                residual(2 * j, j, 0)
                scan(j, i, epar, "e2", "mask2_in")
                back2(2 * j, 0)
                residual(2 * j + 1, j, 1)
                edge_out(j)
                back2(2 * j + 1, 1)

            step2(0, 0, 0)
            step2(1, 0, 1)
            with dve.Fori(1, (EG - 2) // 2) as i:
                own.enter(i - 1, 4)
                step2(2 * i, i, 0)
                step2(2 * i + 1, i, 1)
            own.leave((EG - 2) // 2 - 1)
            residual(NG - 1, NG // 2, 0)
            scan(EG - 2, EG // 2 - 1, 0, "e2", "mask2_in")
            back2(NG - 1, 0)
            edge_out(EG - 2)
            scan(EG - 1, EG // 2 - 1, 1, "e2", "mask2_in")
            edge_out(EG - 1)

            dve.wait_ge(S["e2_evac"], 2 * EG)

            def stage(i):
                for par in range(2):
                    wait(dve, S["e2_add"][par], 16 * K * i)
                    V.tensor_copy(msg[:, par, :, :], msg2[:, bass.ds((2 * i + par) * K, K), :]).then_inc(S["staged"], 1)

            stage(0)
            with dve.Fori(1, EG // 2) as i:
                stage(i)

        @block.scalar
        def _(act):
            A = nc.scalar

            def front1(g, par):
                act.wait_ge(S["d1_mean"], g + 1)
                A.activation(d_sd[:, par, :], d_mv[:, par, :, 1], ACT.Sqrt, bias=eps[:, :]).then_inc(S["d1_std"], 1)
                wait(act, S["d1_T"], 2 * g - 2)
                for h in range(2):
                    for k in range(HT * h, HT * h + HT):
                        ins = A.activation(dh[:, par, k, :], dx[:, par, k, :], ACT.Relu, bias=d_neg[:, par, k:k + 1])
                    ins.then_inc(S["d1_relu"], 1)

            def back(L, g, par, func):
                for h in range(2):
                    act.wait_ge(S[L + "_T"], 2 * g + h + 1)
                    wait(act, S[L + "_M"], 2 * g + h - 3)
                    A.activation(dT[:, par, h * HC:(h + 1) * HC], Td[h][:, :], func).then_inc(S[L + "_hT"], 1)

            def pair1(i):
                front1(2 * i + 1, 1)
                back("d1", 2 * i, 0, ACT.Copy)
                front1(2 * i + 2, 0)
                back("d1", 2 * i + 1, 1, ACT.Copy)

            front1(0, 0)
            pair1(0)
            with act.Fori(1, NG // 2) as i:
                pair1(i)
            back("d1", NG - 1, 0, ACT.Copy)

            def edges1(i):
                for par in range(2):
                    e = 2 * i + par
                    act.wait_ge(S["e1_mean"], e + 1)
                    A.activation(e_sd[:, par, :], e_mv[:, par, :, 1], ACT.Sqrt, bias=eps[:, :]).then_inc(S["e1_std"], 1)
                    act.wait_ge(S["e1_par"], e + 1)
                    wait(act, S["e1_T"], 2 * e - 2)
                    for h in range(2):
                        for k in range(HT * h, HT * h + HT):
                            ins = A.activation(eh[:, par, k, :], eg[:, par, k, :], ACT.Relu,
                                               bias=e_neg[:, par, k:k + 1], scale=e_rs[:, par, k:k + 1])
                        ins.then_inc(S["e1_relu"], 1)

            edges1(0)
            with act.Fori(1, EG // 2) as i:
                edges1(i)

            def edge2(e, i, par):
                act.wait_ge(S["e2_in"][par], 16 * K * (i + 1))
                wait(act, S["e2_T"], 2 * e - 2)
                A.activation(flat(eh, par), flat(eg, par), ACT.Relu).then_inc(S["e2_relu"], 1)

            def step2(j, i, epar):
                edge2(j, i, epar)
                back("d2", 2 * j, 0, ACT.Relu)
                back("d2", 2 * j + 1, 1, ACT.Relu)

            act.wait_ge(S["d1_M"], 2 * NG)
            act.wait_ge(S["e1_T"], 2 * EG)
            step2(0, 0, 0)
            step2(1, 0, 1)
            with act.Fori(1, (EG - 2) // 2) as i:
                step2(2 * i, i, 0)
                step2(2 * i + 1, i, 1)
            edge2(EG - 2, EG // 2 - 1, 0)
            back("d2", NG - 1, 0, ACT.Relu)
            edge2(EG - 1, EG // 2 - 1, 1)

        @block.tensor
        def _(pe):
            T = nc.tensor

            def turn(t, par, h, bank):
                for k in range(HT):
                    ins = T.transpose(bank[:, k * P:(k + 1) * P], t[:, par, HT * h + k, :], ident[:, :])
                return ins

            def dense_T(L, g, par, i):
                for h in range(2):
                    if L == "d1":
                        pe.wait_ge(S["d1_relu"], 2 * g + h + 1)
                    else:
                        pe.wait_ge(S["d2_in"][par], 32 * (i + 1))
                    wait(pe, S[L + "_hT"], 2 * g + h - 1)
                    turn(dh, par, h, Td[h]).then_inc(S[L + "_T"], 1)

            def dense_M(L, g, par, root):
                for h in range(2):
                    pe.wait_ge(S[L + "_hT"], 2 * g + h + 1)
                    wait(pe, S[L + "_evac"], 2 * g + h - 1)
                    for k in range(HT):
                        ins = T.matmul(Md[h][:, k * C:(k + 1) * C], dT[:, par, (HT * h + k) * P:(HT * h + k + 1) * P],
                                       root[:, :], start=True, stop=True)
                    ins.then_inc(S[L + "_M"], 1)

            def edge_T(L, e, par):
                for h in range(2):
                    pe.wait_ge(S[L + "_relu"], 2 * e + h + 1 if L == "e1" else e + 1)
                    wait(pe, S[L + "_scan"], 2 * e + h - 1)
                    turn(eh, par, h, Te[h]).then_inc(S[L + "_T"], 1)

            def edge_M(L, e, par, w):
                for h in range(2):
                    cols = [pe.value_load(wcol[0:1, bass.ds(K * e + HT * h + k, 1)], min_val=0, max_val=(R - 1) * C)
                            for k in range(HT)]
                    pe.wait_ge(S[L + "_scan"], 2 * e + h + 1)
                    wait(pe, S[L + "_evac"], 2 * e + h - 1)
                    for k in range(HT):
                        ins = T.matmul(Me[h][:, k * C:(k + 1) * C], sums[:, par, (HT * h + k) * P:(HT * h + k + 1) * P],
                                       w[:, bass.ds(cols[k], C)], start=True, stop=True)
                    ins.then_inc(S[L + "_M"], 1)

            pe.wait_ge(S["made"], 1)
            pe.wait_ge(S["rec_ready"], 1)
            T.matmul(Me[0][:, 0:R], tri[:, :], n_f, start=True, stop=True)
            T.matmul(Me[0][:, R:2 * R], ones[:, :], n_f, start=True, stop=True).then_inc(S["offs"], 1)

            pe.wait_ge(S["consts_in"], 96)

            def pair1(i):
                dense_T("d1", 2 * i + 1, 1, i)
                dense_M("d1", 2 * i, 0, r1)
                dense_T("d1", 2 * i + 2, 0, i)
                dense_M("d1", 2 * i + 1, 1, r1)

            dense_T("d1", 0, 0, 0)
            pair1(0)
            with pe.Fori(1, NG // 2) as i:
                pair1(i)
            dense_M("d1", NG - 1, 0, r1)

            pe.wait_ge(S["d1_hT"], 2 * NG)
            pe.wait_ge(S["tops_in"], 1)
            for h in range(2):
                T.transpose(Td[0][0:1, h * HR:(h + 1) * HR], begun[0:HR, h, P - 1:P], ident[0:HR, 0:HR])
            for h in range(2):
                ins = T.transpose(Td[1][0:1, h * HR:(h + 1) * HR], rel_rf[0:HR, h:h + 1], ident[0:HR, 0:HR])
            ins.then_inc(S["tops_t"], 1)
            pe.wait_ge(S["tops_in"], 2)
            for h in range(2):
                ins = T.transpose(Te[0][0:HR, h:h + 1], top_sum[0:1, h * HR:(h + 1) * HR], ident[0:1, 0:1])
            ins.then_inc(S["tops_b"], 1)
            pe.wait_ge(S["tops_in"], 3)
            for h in range(2):
                for bank, a in ((Td[0], cur[0:HR, h, :, 0]), (Td[1], aim[0:HR, h, :]), (Te[1], recip[0:HR, h, :])):
                    ins = T.transpose(bank[:, h * HR:(h + 1) * HR], a, ident[0:HR, 0:HR])
            ins.then_inc(S["metaT"], 1)
            pe.wait_ge(S["meta"], 2)

            def edges1(i):
                for par in range(2):
                    edge_T("e1", 2 * i + par, par)
                    edge_M("e1", 2 * i + par, par, w1)

            edges1(0)
            with pe.Fori(1, EG // 2) as i:
                edges1(i)

            def step2(j, epar):
                edge_T("e2", j, epar)
                dense_T("d2", 2 * j + 1, 1, j)
                dense_M("d2", 2 * j, 0, r2)
                edge_M("e2", j, epar, w2)
                dense_T("d2", 2 * j + 2, 0, j + 1)
                dense_M("d2", 2 * j + 1, 1, r2)

            dense_T("d2", 0, 0, 0)
            step2(0, 0)
            step2(1, 1)
            with pe.Fori(1, (EG - 2) // 2) as i:
                step2(2 * i, 0)
                step2(2 * i + 1, 1)
            edge_T("e2", EG - 2, 0)
            dense_M("d2", NG - 1, 0, r2)
            edge_M("e2", EG - 2, 0, w2)
            edge_T("e2", EG - 1, 1)
            edge_M("e2", EG - 1, 1, w2)


_NAMES = {"x": "x", "src": "src", "dst": "dst", "attr": "edge_attr_42",
          "w_rel1": "L0_gnn_w_rel1", "root1": "L0_gnn_root1", "b1": "L0_gnn_b1",
          "w_rel2": "L0_gnn_w_rel2", "root2": "L0_gnn_root2", "b2": "L0_gnn_b2"}


def kernel(**inputs):
    import numpy as np
    import concourse.bacc as bacc
    from concourse.bass_utils import run_bass_kernel_spmd

    nc = bacc.Bacc("TRN2", target_bir_lowering=False, num_devices=1)
    arrays, args = {}, []
    for short, name in _NAMES.items():
        a = np.ascontiguousarray(inputs[name])
        if short in ("src", "dst"):
            a = a.reshape(-1, 1)
        arrays[f"in_{short}"] = a
        args.append(nc.dram_tensor(f"in_{short}", a.shape, mybir.dt.from_np(a.dtype), kind="ExternalInput").ap())
    args.append(nc.dram_tensor("out_rows", (N + SPARE, C), F32, kind="ExternalOutput").ap())
    build(nc, *args)
    r = run_bass_kernel_spmd(nc, [arrays], core_ids=[0])
    return r.results[0]["out_rows"][:N]
```

```python
import concourse.bass as bass
from concourse import mybir
from contextlib import ExitStack

F32, I32, U8 = mybir.dt.float32, mybir.dt.int32, mybir.dt.uint8
ALU, ACT, AX = mybir.AluOpType, mybir.ActivationFunctionType, mybir.AxisListType

P = 128
N, C, E, R = 50000, 128, 25000, 10
ATTR, REL0 = 42, 16
EPS = 1e-5
K = 8
HT = K // 2
HC = HT * C
GROUP = K * P
J = -(-E // P)
TAIL_P, TAIL_J = E // J, E % J
NG = -(-N // GROUP)
TILES = -(-((E + R * (P - 1)) // P) // K) * K
EG = TILES // K
SLOTS = TILES * P
HR = TILES // 2
SPARE = 2 * GROUP
KEY = 1 << 16
PADKEY = R * KEY
TROWS = -(-(SLOTS + 2) // P) * P
SKIP = 1 << 20
SCAT = 14
assert J % (2 * SCAT) == 0 and NG % 2 == 1 and EG % 2 == 0 and 2 * (EG - 2) == NG - 1 and HR <= P


def wait(eng, sem, value):
    if not (isinstance(value, int) and value <= 0):
        eng.wait_ge(sem, value)


def alone(eng, ticks):
    eng.sem_inc(ticks, 1)


class Own:

    def __init__(self, eng, sem):
        self.eng, self.sem, self.base, self.n = eng, sem, 0, 0

    def done(self, ins):
        ins.then_inc(self.sem, 1)
        self.n += 1
        self.eng.wait_ge(self.sem, self.base + self.n)

    def enter(self, i, per):
        self.start = self.base + self.n if self.n or isinstance(self.base, int) else self.start
        self.base, self.per, self.n = self.start + i * per, per, 0

    def leave(self, times):
        assert self.n == self.per, (self.n, self.per)
        self.base, self.n = self.start + times * self.per, 0


def build(nc, x, src, dst, attr, w_rel1, root1, b1, w_rel2, root2, b2, out):
    ctx = ExitStack()
    with ctx:
        def sb(name, shape, dt=F32):
            return ctx.enter_context(nc.sbuf_tensor(name, shape, dt))

        def sem(name):
            return ctx.enter_context(nc.semaphore(name))

        def dram(name, shape, dt=F32):
            return nc.dram_tensor(name, shape, dt, kind="Internal").ap()

        pre1 = dram("pre1", (N + SPARE, C))
        table = dram("slot_table", (TROWS, 2))
        mask_d = dram("mask_d", (TILES, P), U8)

        w_all = sb("w_all", [P, (R + 16) * C])
        w1, w2 = w_all[:, 0:R * C], w_all[:, R * C:2 * R * C]
        r1, r2 = sb("r1", [P, C]), sb("r2", [P, C])
        b1c, b2b = sb("b1c", [P, 1]), sb("b2b", [P, C])
        ident, tri, ones = sb("ident", [P, P]), sb("tri", [P, P]), sb("ones", [P, P])
        eps = sb("eps", [P, 1])

        msg2 = sb("msg2", [P, TILES, C])
        scratch = msg2[:, :, :].rearrange("p t c -> p (t c)")
        at = [0]

        def carve(n, dt=F32):
            at[0] += n
            assert at[0] <= TILES * C
            v = scratch[:, at[0] - n:at[0]]
            return v if dt is F32 else v.bitcast(dt)

        attr_s = carve(J * ATTR).rearrange("p (j a) -> p j a", a=ATTR)
        cand = carve(J * R).rearrange("p (j r) -> p j r", r=R)
        hot = carve(R * J).rearrange("p (r j) -> p r j", r=R)
        goes_on = carve(R * J).rearrange("p (r j) -> p r j", r=R)
        rank = carve(R * J).rearrange("p (r j) -> p r j", r=R)
        src_i0, dst_i0 = carve(J, I32), carve(J, I32)
        e_no, best, rel, void = carve(J), carve(J), carve(J), carve(J)
        row_f, row_i = carve(J), carve(J, I32)
        rec = carve(J * 2).rearrange("p (j c) -> p j c", c=2)
        r_no = carve(R)
        both = carve(2 * R)
        n_i, n_f, n_sum, shift = carve(R, I32), carve(R), carve(R), carve(R)
        fill = carve(TROWS // P * 2).rearrange("p (j c) -> p j c", c=2)
        zeros = carve(SPARE // P * C)

        def halves(dt=F32):
            return carve(2 * P, dt).rearrange("p (h i) -> p h i", h=2)

        s_no, s_i = halves(), halves(I32)
        at[0] = 0
        cur = carve(2 * P * 2).rearrange("p (h i c) -> p h i c", h=2, c=2)
        prev = carve(2 * P * 2).rearrange("p (h i c) -> p h i c", h=2, c=2)
        nxt = carve(2 * P * 2).rearrange("p (h i c) -> p h i c", h=2, c=2)

        same, last, first, begun, count, recip, node, spare, aim = (halves() for _ in range(9))
        key_i, node_i = halves(I32), halves(I32)
        carry = carve(2)
        rel_ri, rel_rf = carve(2, I32), carve(2)
        tops, top_sum = carve(TILES + 1), carve(TILES + 1)
        rel_c, power, flag = carve(TILES), carve(TILES), carve(TILES)
        flag_f, packed, packed_f = carve(EG), carve(TILES), carve(TILES // HT)

        same_b = sb("same_b", [P, 2, P], U8)
        src_all, aim_all = sb("src_all", [P, TILES], I32), sb("aim_all", [P, TILES], I32)
        rc_all = sb("rc_all", [P, TILES])
        rels = sb("rels", [1, TILES // HT], I32)
        starts = sb("starts", [1, EG], I32)

        stage_i = sb("stage_i", [P, 2, SCAT], I32)
        stage_r = sb("stage_r", [P, 2, SCAT, 2])
        g_idx, s_idx = sb("g_idx", [P, 2, K], I32), sb("s_idx", [P, 2, K], I32)
        eg, eh = sb("eg", [P, 2, K, C]), sb("eh", [P, 2, K, C])
        ehT = eh[:, :, :, :].rearrange("p a k c -> p a (k c)")
        sums = sb("sums", [P, 2, GROUP])
        mask = sb("mask", [P, 2, GROUP], U8)
        msg = sb("msg", [P, 2, K, C])
        dx = sb("dx", [P, 2, K, C])
        dh = sb("dh", [P, 2, K, C])
        dT = sb("dT", [P, 2, GROUP])
        do = sb("do", [P, 2, K, C])
        d_st, e_st = sb("d_st", [P, K, 6]), sb("e_st", [P, K, 6])
        d_mv, e_mv = sb("d_mv", [P, 2, K, 2]), sb("e_mv", [P, 2, K, 2])
        d_neg, d_sd, d_rs = sb("d_neg", [P, 2, K]), sb("d_sd", [P, 2, K]), sb("d_rs", [P, 2, K])
        e_neg, e_sd, e_rs = sb("e_neg", [P, 2, K]), sb("e_sd", [P, 2, K]), sb("e_rs", [P, 2, K])

        ps = [ctx.enter_context(nc.psum_tensor(f"bank{n}", [P, HC], F32)) for n in range(8)]
        Td, Te, Md, Me = ps[0:2], ps[2:4], ps[4:6], ps[6:8]

        S = {}
        for name in ("attr_in ids_in consts_in made pads_set filled spare_zero rec_ready offs sorted "
                     "m_in tops_t tops_in tops_b metaT mask_out meta gidx_set "
                     "d1_mean d1_std d1_relu d1_T d1_hT d1_M d1_evac "
                     "e1_mean e1_std e1_par e1_relu e1_T e1_scan e1_M e1_evac "
                     "d2_T d2_hT d2_M d2_evac e2_relu e2_T e2_scan e2_M e2_evac staged "
                     "dve_own pool_own dve_ticks pool_ticks").split():
            S[name] = sem(name)
        for name in "rec_out d1_in d1_stored e1_in mask_in e1_add d2_p d2_x d2_stored e2_in mask2_in e2_add".split():
            S[name] = [sem(f"{name}{n}") for n in range(2)]

        block = ctx.enter_context(nc.Block())

        def rows(a, g):
            base = g * GROUP if not isinstance(g, int) else min(g * GROUP, N - GROUP)
            return a[bass.ds(base, GROUP), :].rearrange("(p k) c -> p (k c)", k=K)

        def flat(t, par):
            return t[:, par, :, :].rearrange("p k c -> p (k c)")

        def shifted(by):
            return [table[by + h * HR * P:by + (h + 1) * HR * P, :].rearrange("(t i) c -> t (i c)", i=P)
                    for h in range(2)]

        @block.sync
        def _(sp):
            whole = TAIL_P // 16 * 16
            sp.wait_ge(S["pads_set"], 1)
            for a, t, w, done in ((attr, attr_s.rearrange("p j a -> p (j a)"), ATTR, "attr_in"),
                                  (src, src_i0, 1, "ids_in"), (dst, dst_i0, 1, "ids_in")):
                v = a[0:TAIL_P * J].rearrange("(p j) a -> p (j a)", j=J)
                sp.dma_start(t[0:whole, :], v[0:whole, :]).then_inc(S[done], 16)
                sp.dma_start(t[whole:TAIL_P, :], v[whole:TAIL_P, :]).then_inc(S[done], 16)
                tail = a[TAIL_P * J:E].rearrange("(p j) a -> p (j a)", p=1)
                sp.dma_start(t[TAIL_P:TAIL_P + 1, 0:TAIL_J * w], tail).then_inc(S[done], 16)
            sp.dma_start(table.rearrange("(p j) c -> p (j c)", p=P),
                         fill.rearrange("p j c -> p (j c)")).then_inc(S["filled"], 16)
            for t in (pre1, out):
                sp.dma_start(t[N:N + SPARE, :].rearrange("(p k) c -> p (k c)", p=P),
                             zeros).then_inc(S["spare_zero"], 16)
            for t, a in ((w1, w_rel1), (w2, w_rel2)):
                sp.dma_start(t.rearrange("c (r o) -> c r o", r=R),
                             a.rearrange("r c o -> c r o")).then_inc(S["consts_in"], 16)
            for t, a in ((r1, root1), (r2, root2), (b1c, b1.unsqueeze(1)),
                         (b2b, b2.partition_broadcast(P))):
                sp.dma_start(t[:, :], a).then_inc(S["consts_in"], 16)

            def load1(g, i, par):
                wait(sp, S["d1_relu"], 2 * g - 2)
                sp.dma_start(flat(dx, par), rows(x, g)).then_inc(S["d1_in"][par], 16)

            def store1(g, par):
                sp.wait_ge(S["d1_evac"], 2 * g + 2)
                sp.dma_start(rows(pre1, g), flat(do, par)).then_inc(S["d1_stored"][par], 16)

            def pair1(i):
                load1(2 * i + 2, i, 0)
                store1(2 * i, 0)
                load1(2 * i + 3, i, 1)
                store1(2 * i + 1, 1)

            load1(0, 0, 0)
            load1(1, 0, 1)
            pair1(0)
            with sp.Fori(1, NG // 2 - 1) as i:
                pair1(i)
            load1(NG - 1, 0, 0)
            store1(NG - 3, 0)
            store1(NG - 2, 1)
            sp.wait_ge(S["d1_stored"][1], 16 * (NG // 2))
            store1(NG - 1, 0)

            for par in range(2):
                sp.wait_ge(S["rec_out"][par], 16 * J // 2)
            for t, by in ((cur, 1), (prev, 0), (nxt, 2)):
                for h, v in enumerate(shifted(by)):
                    sp.dma_start(t[0:HR, h].rearrange("p i c -> p (i c)"), v).then_inc(S["m_in"], 16)
            sp.wait_ge(S["meta"], 1)
            for h in range(2):
                sp.dma_start(mask_d[h * HR:(h + 1) * HR, :], same_b[0:HR, h, :]).then_inc(S["mask_out"], 16)
            sp.wait_ge(S["mask_out"], 32)

            def load_mask(e, par, scan, done):
                wait(sp, S[scan], 2 * e - 2)
                v = mask_d[bass.ds(e * K, K), :].rearrange("t i -> (t i)").partition_broadcast(P)
                sp.dma_start(mask[:, par, :], v).then_inc(S[done][par], 16)

            def masks1(i):
                for par in range(2):
                    load_mask(2 * i + par, par, "e1_scan", "mask_in")

            masks1(0)
            with sp.Fori(1, EG // 2) as i:
                masks1(i)

            for par in range(2):
                sp.wait_ge(S["e1_add"][par], 16 * K * EG // 2)

            def load_p(g, par):
                wait(sp, S["d2_T"], 2 * g - 2)
                sp.dma_start(flat(dh, par), rows(pre1, g)).then_inc(S["d2_p"][par], 16)

            def load_x(g, par):
                wait(sp, S["d2_evac"], 2 * g - 2)
                sp.dma_start(flat(dx, par), rows(x, g)).then_inc(S["d2_x"][par], 16)

            def store2(g, par):
                sp.wait_ge(S["d2_evac"], 2 * g + 2)
                sp.dma_start(rows(out, g), flat(do, par)).then_inc(S["d2_stored"][par], 16)

            def step2(j, epar, more):
                load_p(2 * j + 2, 0)
                store2(2 * j, 0)
                load_x(2 * j + 2, 0)
                load_mask(j + 1, 1 - epar, "e2_scan", "mask2_in")
                if more:
                    load_p(2 * j + 3, 1)
                store2(2 * j + 1, 1)
                if more:
                    load_x(2 * j + 3, 1)

            load_mask(0, 0, "e2_scan", "mask2_in")
            for par in range(2):
                load_p(par, par)
                load_x(par, par)
            step2(0, 0, True)
            step2(1, 1, True)
            with sp.Fori(1, (EG - 2) // 2 - 1) as i:
                step2(2 * i, 0, True)
                step2(2 * i + 1, 1, True)
            step2(EG - 4, 0, True)
            step2(EG - 3, 1, False)
            load_mask(EG - 1, 1, "e2_scan", "mask2_in")
            sp.wait_ge(S["d2_stored"][1], 16 * (NG // 2))
            store2(NG - 1, 0)
            sp.wait_ge(S["d2_stored"][0], 16 * (NG // 2 + 1))

        @block.gpsimd
        def _(pool):
            own = Own(pool, S["pool_own"])
            pool.memset(ident[:, :], 0.0)
            own.done(pool.memset(ones[:, :], 1.0))
            pool.affine_select(out=ident[:, :], in_=ident[:, :], compare_op=ALU.not_equal, fill=1.0,
                               base=0, pattern=[[-1, P]], channel_multiplier=1)
            pool.affine_select(out=tri[:, :], in_=ones[:, :], compare_op=ALU.is_gt, fill=0.0,
                               base=0, pattern=[[1, P]], channel_multiplier=-1)
            pool.iota(e_no, pattern=[[1, J]], base=0, channel_multiplier=J,
                      allow_small_or_imprecise_dtypes=True)
            pool.iota(r_no, pattern=[[1, R]], base=0, channel_multiplier=0,
                      allow_small_or_imprecise_dtypes=True)
            pool.iota(s_no[0:HR], pattern=[[HR * P, 2], [1, P]], base=0, channel_multiplier=P,
                      allow_small_or_imprecise_dtypes=True)
            pool.iota(s_i[0:HR], pattern=[[HR * P, 2], [1, P]], base=0,
                      channel_multiplier=P).then_inc(S["made"], 1)

            pool.wait_ge(S["filled"], 16)
            pool.wait_ge(S["sorted"], 1)

            def scatter_records(i):
                for par in range(2):
                    j0 = (2 * i + par) * SCAT
                    wait(pool, S["rec_out"][par], 16 * SCAT * i)
                    pool.tensor_copy(stage_i[:, par, :], row_i[:, bass.ds(j0, SCAT)])
                    own.done(pool.tensor_copy(stage_r[:, par, :, :], rec[:, bass.ds(j0, SCAT), :]))
                    alone(pool, S["pool_ticks"])
                    for k in range(SCAT):
                        pool.indirect_dma_start(
                            table, bass.IndirectOffsetOnAxis(ap=stage_i[:, par, k:k + 1], axis=0),
                            stage_r[:, par, k, :], None, bounds_check=TROWS - 1,
                            oob_is_err=False).then_inc(S["rec_out"][par], 16)

            scatter_records(0)
            with pool.Fori(1, J // (2 * SCAT)) as i:
                own.enter(i - 1, 2)
                scatter_records(i)
            own.leave(J // (2 * SCAT) - 1)

            def gather(table_, e, i, par, free, done):
                wait(pool, S[free], 2 * e - 2)
                own.done(pool.tensor_copy(g_idx[:, par, :], src_all[:, bass.ds(e * K, K)]))
                alone(pool, S["pool_ticks"])
                for k in range(K):
                    pool.indirect_dma_start(
                        eg[:, par, k, :], None, table_,
                        bass.IndirectOffsetOnAxis(ap=g_idx[:, par, k:k + 1], axis=0)
                    ).then_inc(S[done][par], 16)

            def scatter_add(table_, e, i, par, done):
                wait(pool, S[done][par], 16 * K * i)
                own.done(pool.tensor_copy(s_idx[:, par, :], aim_all[:, bass.ds(e * K, K)]))
                alone(pool, S["pool_ticks"])
                bits = pool.value_load(starts[0:1, bass.ds(e, 1)], min_val=0, max_val=(1 << K) - 1)

                def add(k):
                    pool.indirect_dma_start(
                        table_, bass.IndirectOffsetOnAxis(ap=s_idx[:, par, k:k + 1], axis=0),
                        msg[:, par, k, :], None, compute_op=ALU.add).then_inc(S[done][par], 16)

                def all_earlier(k):
                    wait(pool, S[done][par], 16 * (K * i + k))
                    wait(pool, S[done][1 - par], 16 * K * (i + par))
                    alone(pool, S["pool_ticks"])

                with pool.If(bits):
                    for k in range(K):
                        with pool.If(bits & (1 << k)):
                            all_earlier(k)
                        add(k)
                with pool.Else():
                    for k in range(K):
                        add(k)

            pool.wait_ge(S["meta"], 2)

            def pair1(i, more=True):
                for par in range(2):
                    if more:
                        gather(x, 2 * i + par + 2, i, par, "e1_relu", "e1_in")
                    if isinstance(i, int) and i == 0 and par == 0:
                        pool.wait_ge(S["spare_zero"], 32)
                        pool.wait_ge(S["d1_stored"][0], 16 * (NG // 2 + 1))
                        pool.wait_ge(S["d1_stored"][1], 16 * (NG // 2))
                    pool.wait_ge(S["e1_evac"], 2 * (2 * i + par) + 2)
                    scatter_add(pre1, 2 * i + par, i, par, "e1_add")

            for par in range(2):
                gather(x, par, 0, par, "e1_relu", "e1_in")
            pair1(0)
            with pool.Fori(1, EG // 2 - 1) as i:
                own.enter(i - 1, 4)
                pair1(i)
            own.leave(EG // 2 - 2)
            pair1(EG // 2 - 1, more=False)

            for par in range(2):
                pool.wait_ge(S["e1_add"][par], 16 * K * EG // 2)

            def gathers2(i):
                for par in range(2):
                    gather(pre1, 2 * i + par, i, par, "e2_T", "e2_in")

            gathers2(0)
            with pool.Fori(1, EG // 2) as i:
                own.enter(i - 1, 2)
                gathers2(i)
            own.leave(EG // 2 - 1)

            pool.wait_ge(S["d2_stored"][0], 16 * (NG // 2 + 1))
            pool.wait_ge(S["d2_stored"][1], 16 * (NG // 2))

            def adds2(i):
                for par in range(2):
                    pool.wait_ge(S["staged"], 2 * i + par + 1)
                    scatter_add(out, 2 * i + par, i, par, "e2_add")

            adds2(0)
            with pool.Fori(1, EG // 2) as i:
                own.enter(i - 1, 2)
                adds2(i)
            own.leave(EG // 2 - 1)
            for par in range(2):
                pool.wait_ge(S["e2_add"][par], 16 * K * EG // 2)

        @block.vector
        def _(dve):
            own = Own(dve, S["dve_own"])
            V = nc.vector
            q = TAIL_P // 32 * 32
            V.memset(attr_s[q:P, TAIL_J:J, REL0:REL0 + R], 0.0)
            V.memset(src_i0[q:P, TAIL_J:J], 0)
            V.memset(dst_i0[q:P, TAIL_J:J], 0)
            V.memset(zeros, 0.0)
            V.memset(fill[:, :, 0], 0.0)
            V.memset(eps[:, :], EPS)
            V.memset(fill[:, :, 1], float(PADKEY)).then_inc(S["pads_set"], 1)
            own.done(V.memset(goes_on, 1.0))
            own.done(V.memset(goes_on[:, :, 0], 0.0))

            dve.wait_ge(S["made"], 1)
            dve.wait_ge(S["attr_in"], 48)
            scores = attr_s[:, :, REL0:REL0 + R]
            own.done(V.tensor_reduce(best, scores, axis=AX.X, op=ALU.max))
            own.done(V.tensor_tensor(cand, scores, best.unsqueeze(2).to_broadcast([P, J, R]), ALU.is_equal))
            own.done(V.scalar_tensor_tensor(cand, cand, -float(R), r_no.unsqueeze(1).to_broadcast([P, J, R]),
                                            ALU.mult, ALU.add))
            own.done(V.tensor_reduce(rel, cand, axis=AX.X, op=ALU.min))
            V.tensor_scalar(rel, rel, float(R), None, ALU.add)
            own.done(V.tensor_scalar(void, e_no, float(E), None, ALU.is_ge))
            own.done(V.scalar_tensor_tensor(rel, void, float(2 * R), rel, ALU.mult, ALU.add))
            own.done(V.tensor_tensor(hot, rel.unsqueeze(1).to_broadcast([P, R, J]),
                                     r_no.unsqueeze(2).to_broadcast([P, R, J]), ALU.is_equal))
            own.done(V.tensor_tensor_scan(rank.rearrange("p r j -> p (r j)"),
                                          goes_on.rearrange("p r j -> p (r j)"),
                                          hot.rearrange("p r j -> p (r j)"), 0.0, ALU.mult, ALU.add))
            V.tensor_copy(n_f, rank[:, :, J - 1]).then_inc(S["rec_ready"], 1)
            dve.wait_ge(S["ids_in"], 96)
            V.tensor_copy(rec[:, :, 0], src_i0)
            own.done(V.tensor_copy(row_f, dst_i0))
            own.done(V.scalar_tensor_tensor(rec[:, :, 1], rel, float(KEY), row_f, ALU.mult, ALU.add))
            dve.wait_ge(S["offs"], 1)
            own.done(V.tensor_copy(both, Me[0][:, 0:2 * R]))
            own.done(V.tensor_scalar(n_i, both[:, R:2 * R], float(P - 1), None, ALU.add))
            own.done(V.tensor_scalar(n_i, n_i, 7, None, ALU.logical_shift_right))
            own.done(V.tensor_copy(n_f, n_i))
            own.done(V.tensor_tensor_scan(n_sum, ones[:, 0:R], n_f, 0.0, ALU.mult, ALU.add))
            own.done(V.tensor_tensor(n_sum, n_sum, n_f, ALU.subtract))
            own.done(V.scalar_tensor_tensor(shift, n_sum, float(P), both[:, 0:R], ALU.mult, ALU.add))
            own.done(V.tensor_tensor(rank, rank, shift.unsqueeze(2).to_broadcast([P, R, J]), ALU.add))
            own.done(V.tensor_tensor(rank, rank, hot, ALU.mult))
            own.done(V.tensor_reduce(row_f, rank.rearrange("p r j -> p j r"), axis=AX.X, op=ALU.add))
            own.done(V.scalar_tensor_tensor(row_f, void, float(SKIP), row_f, ALU.mult, ALU.add))
            V.tensor_copy(row_i, row_f).then_inc(S["sorted"], 1)

            def stats(t, par, st, mv):
                for k in range(K):
                    ins = V.bn_stats(st[:, k, :], t[:, par, k, :])
                own.done(ins)
                alone(dve, S["dve_ticks"])
                for k in range(K):
                    ins = V.bn_aggr(mv[:, par, k, :], st[:, k, :])
                return ins

            def front1(g, i, par):
                dve.wait_ge(S["d1_in"][par], 16 * (i + 1))
                wait(dve, S["d1_relu"], 2 * g - 2)
                own.done(stats(dx, par, d_st, d_mv))
                V.tensor_scalar(d_neg[:, par, :], d_mv[:, par, :, 0], -1.0, None,
                                ALU.mult).then_inc(S["d1_mean"], 1)

            def back1(g, i, par):
                dve.wait_ge(S["d1_std"], g + 1)
                own.done(V.reciprocal(d_rs[:, par, :], d_sd[:, par, :]))
                wait(dve, S["d1_stored"][par], 16 * i)
                for h in range(2):
                    dve.wait_ge(S["d1_M"], 2 * g + h + 1)
                    rs = d_rs[:, par, HT * h:HT * h + HT].unsqueeze(2).to_broadcast([P, HT, C])
                    V.tensor_tensor(do[:, par, HT * h:HT * h + HT, :], Md[h][:, :].rearrange("p (k c) -> p k c", c=C),
                                    rs, ALU.mult).then_inc(S["d1_evac"], 1)

            def pair1(i, last=False):
                front1(2 * i + 1, i, 1)
                back1(2 * i, i, 0)
                front1(2 * i + 2, i + 1, 0)
                back1(2 * i + 1, i, 1)

            dve.wait_ge(S["consts_in"], 96)
            front1(0, 0, 0)
            pair1(0)
            with dve.Fori(1, NG // 2) as i:
                own.enter(i - 1, 6)
                pair1(i)
            own.leave(NG // 2 - 1)
            back1(NG - 1, NG // 2, 0)

            dve.wait_ge(S["m_in"], 96)
            key = cur[0:HR, :, :, 1]
            r = slice(0, HR)
            V.tensor_tensor(same[r], key, prev[r, :, :, 1], ALU.is_equal)
            V.tensor_tensor(last[r], key, nxt[r, :, :, 1], ALU.not_equal)
            V.tensor_copy(key_i[r], key)
            V.tensor_scalar(first[r], key, float(PADKEY), None, ALU.is_lt)
            own.done(V.tensor_scalar(node_i[r], s_i[r], SPARE - 1, None, ALU.bitwise_and))
            V.tensor_copy(same_b[r], same[r]).then_inc(S["meta"], 1)
            V.tensor_tensor(last[r], last[r], first[r], ALU.mult)
            V.tensor_copy(spare[r], node_i[r])
            own.done(V.tensor_scalar(rel_ri[r], key_i[r, :, 0], 16, None, ALU.logical_shift_right))
            V.tensor_scalar(node_i[r], key_i[r], KEY - 1, None, ALU.bitwise_and)
            V.tensor_scalar(spare[r], spare[r], float(N), None, ALU.add)
            V.tensor_copy(rel_rf[r], rel_ri[r])
            own.done(V.tensor_scalar(first[r], same[r], -1.0, 1.0, ALU.mult, ALU.add))
            V.tensor_scalar(rel_rf[r], rel_rf[r], float(R - 1), None, ALU.min)
            V.tensor_copy(node[r], node_i[r])
            own.done(V.tensor_tensor(first[r], first[r], s_no[r], ALU.mult))
            for h in range(2):
                ins = V.tensor_tensor_scan(begun[r, h], first[r, h], first[r, h], 0.0, ALU.max, ALU.max)
            ins.then_inc(S["tops_in"], 1)
            own.done(V.tensor_tensor(node[r], node[r], spare[r], ALU.subtract))
            own.done(V.tensor_tensor(node[r], node[r], last[r], ALU.mult))
            own.done(V.tensor_tensor(aim[r], node[r], spare[r], ALU.add))
            V.memset(tops[0:1, 0:1], 0.0)
            dve.wait_ge(S["tops_t"], 1)
            V.tensor_copy(tops[0:1, 1:TILES + 1], Td[0][0:1, 0:TILES])
            own.done(V.tensor_copy(rel_c[0:1], Td[1][0:1, 0:TILES]))
            V.tensor_tensor_scan(top_sum[0:1], tops[0:1], tops[0:1], 0.0, ALU.max,
                                 ALU.max).then_inc(S["tops_in"], 1)
            for k in range(K):
                V.memset(power[0:1].rearrange("p (g k) -> p g k", k=K)[:, :, k], float(1 << k))
                V.memset(packed[0:1].rearrange("p (g k) -> p g k", k=K)[:, :, k], float(16 ** (k % HT)))
            V.memset(flag[0:1, 0:1], 0.0)
            own.done(V.tensor_tensor(flag[0:1, 1:TILES], rel_c[0:1, 1:TILES], rel_c[0:1, 0:TILES - 1],
                                     ALU.not_equal))
            V.tensor_tensor(packed[0:1], rel_c[0:1], packed[0:1], ALU.mult)
            own.done(V.tensor_tensor(flag[0:1], flag[0:1], power[0:1], ALU.mult))
            own.done(V.tensor_reduce(packed_f[0:1], packed[0:1].rearrange("p (g k) -> p g k", k=HT),
                                     axis=AX.X, op=ALU.add))
            V.tensor_copy(rels[0:1, :], packed_f[0:1])
            own.done(V.tensor_reduce(flag_f[0:1], flag[0:1].rearrange("p (g k) -> p g k", k=K),
                                     axis=AX.X, op=ALU.add))
            V.tensor_copy(starts[0:1, :], flag_f[0:1])
            dve.wait_ge(S["tops_b"], 1)
            own.done(V.tensor_copy(carry[r], Te[0][r, 0:2]))
            own.done(V.tensor_tensor(begun[r], begun[r], carry[r].unsqueeze(2).to_broadcast([HR, 2, P]), ALU.max))
            own.done(V.scalar_tensor_tensor(count[r], s_no[r], 1.0, begun[r], ALU.add, ALU.subtract))
            V.reciprocal(recip[r], count[r]).then_inc(S["tops_in"], 1)
            dve.wait_ge(S["metaT"], 1)
            V.tensor_copy(src_all[:, :], Td[0][:, 0:TILES])
            V.tensor_copy(aim_all[:, :], Td[1][:, 0:TILES])
            V.tensor_copy(rc_all[:, :], Te[1][:, 0:TILES]).then_inc(S["meta"], 1)

            def scan(e, i, par, L, mask_in):
                for h in range(2):
                    dve.wait_ge(S["e1_T" if L == "e1" else "e2_relu"], 2 * e + h + 1)
                    rows_T = Te[h][:, :] if L == "e1" else ehT[:, par, h * HC:(h + 1) * HC]
                    dve.wait_ge(S[mask_in][par], 16 * (i + 1))
                    wait(dve, S[L + "_M"], 2 * e + h - 3)
                    wait(dve, S[L + "_scan"], 2 * e + h)
                    before = sums[:, par, HC - 1:HC] if h else sums[:, 1 - par, GROUP - 1:GROUP]
                    if h == 0 and isinstance(e, int) and e == 0:
                        before = 0.0
                    V.tensor_tensor_scan(sums[:, par, h * HC:(h + 1) * HC], mask[:, par, h * HC:(h + 1) * HC],
                                         rows_T, before, ALU.mult, ALU.add).then_inc(S[L + "_scan"], 1)

            def over_count(e, h, to, L):
                dve.wait_ge(S[L + "_M"], 2 * e + h + 1)
                rc = rc_all[:, bass.ds(K * e + HT * h, HT)].unsqueeze(2).to_broadcast([P, HT, C])
                V.tensor_tensor(to, Me[h][:, :].rearrange("p (k c) -> p k c", c=C), rc,
                                ALU.mult).then_inc(S[L + "_evac"], 1)

            def edges1(i):
                for par in range(2):
                    e = 2 * i + par
                    dve.wait_ge(S["e1_in"][par], 16 * K * (i + 1))
                    wait(dve, S["e1_relu"], 2 * e - 2)
                    stats(eg, par, e_st, e_mv).then_inc(S["e1_mean"], 1)
                    dve.wait_ge(S["e1_std"], e + 1)
                    own.done(V.reciprocal(e_rs[:, par, :], e_sd[:, par, :]))
                    V.scalar_tensor_tensor(e_neg[:, par, :], e_mv[:, par, :, 0], -1.0, e_rs[:, par, :],
                                           ALU.mult, ALU.mult).then_inc(S["e1_par"], 1)
                    scan(e, i, par, "e1", "mask_in")
                    wait(dve, S["e1_add"][par], 16 * K * i)
                    for h in range(2):
                        over_count(e, h, msg[:, par, HT * h:HT * h + HT, :], "e1")

            edges1(0)
            with dve.Fori(1, EG // 2) as i:
                own.enter(i - 1, 4)
                edges1(i)
            own.leave(EG // 2 - 1)

            for par in range(2):
                dve.wait_ge(S["e1_add"][par], 16 * K * EG // 2)

            def residual(g, i, par):
                dve.wait_ge(S["d2_x"][par], 16 * (i + 1))
                wait(dve, S["d2_stored"][par], 16 * i)
                own.done(V.tensor_tensor(do[:, par, :, :], dx[:, par, :, :],
                                         b2b[:, :].unsqueeze(1).to_broadcast([P, K, C]), ALU.add))

            def back2(g, par):
                for h in range(2):
                    dve.wait_ge(S["d2_M"], 2 * g + h + 1)
                    o = flat(do, par)[:, h * HC:(h + 1) * HC]
                    V.tensor_tensor(o, Md[h][:, :], o, ALU.add).then_inc(S["d2_evac"], 1)

            def edge_out(e):
                for h in range(2):
                    over_count(e, h, msg2[:, bass.ds(K * e + HT * h, HT), :], "e2")

            def step2(j, i, epar):
                residual(2 * j, j, 0)
                scan(j, i, epar, "e2", "mask2_in")
                back2(2 * j, 0)
                residual(2 * j + 1, j, 1)
                edge_out(j)
                back2(2 * j + 1, 1)

            step2(0, 0, 0)
            step2(1, 0, 1)
            with dve.Fori(1, (EG - 2) // 2) as i:
                own.enter(i - 1, 4)
                step2(2 * i, i, 0)
                step2(2 * i + 1, i, 1)
            own.leave((EG - 2) // 2 - 1)
            residual(NG - 1, NG // 2, 0)
            scan(EG - 2, EG // 2 - 1, 0, "e2", "mask2_in")
            back2(NG - 1, 0)
            edge_out(EG - 2)
            scan(EG - 1, EG // 2 - 1, 1, "e2", "mask2_in")
            edge_out(EG - 1)

            dve.wait_ge(S["e2_evac"], 2 * EG)

            def stage(i):
                for par in range(2):
                    wait(dve, S["e2_add"][par], 16 * K * i)
                    V.tensor_copy(msg[:, par, :, :], msg2[:, bass.ds((2 * i + par) * K, K), :]).then_inc(S["staged"], 1)

            stage(0)
            with dve.Fori(1, EG // 2) as i:
                stage(i)

        @block.scalar
        def _(act):
            A = nc.scalar

            def front1(g, par):
                act.wait_ge(S["d1_mean"], g + 1)
                A.activation(d_sd[:, par, :], d_mv[:, par, :, 1], ACT.Sqrt, bias=eps[:, :]).then_inc(S["d1_std"], 1)
                wait(act, S["d1_T"], 2 * g - 2)
                for h in range(2):
                    for k in range(HT * h, HT * h + HT):
                        ins = A.activation(dh[:, par, k, :], dx[:, par, k, :], ACT.Relu, bias=d_neg[:, par, k:k + 1])
                    ins.then_inc(S["d1_relu"], 1)

            def back(L, g, par):
                for h in range(2):
                    act.wait_ge(S[L + "_T"], 2 * g + h + 1)
                    wait(act, S[L + "_M"], 2 * g + h - 3)
                    to = dT[:, par, h * HC:(h + 1) * HC]
                    if L == "d1":
                        ins = A.activation(to, Td[h][:, :], ACT.Copy)
                    else:
                        ins = A.activation(to, Td[h][:, :], ACT.Relu, bias=b1c[:, :])
                    ins.then_inc(S[L + "_hT"], 1)

            def pair1(i):
                back("d1", 2 * i, 0)
                front1(2 * i + 1, 1)
                back("d1", 2 * i + 1, 1)
                front1(2 * i + 2, 0)

            front1(0, 0)
            pair1(0)
            with act.Fori(1, NG // 2) as i:
                pair1(i)
            back("d1", NG - 1, 0)

            def edges1(i):
                for par in range(2):
                    e = 2 * i + par
                    act.wait_ge(S["e1_mean"], e + 1)
                    A.activation(e_sd[:, par, :], e_mv[:, par, :, 1], ACT.Sqrt, bias=eps[:, :]).then_inc(S["e1_std"], 1)
                    act.wait_ge(S["e1_par"], e + 1)
                    wait(act, S["e1_T"], 2 * e - 2)
                    for h in range(2):
                        for k in range(HT * h, HT * h + HT):
                            ins = A.activation(eh[:, par, k, :], eg[:, par, k, :], ACT.Relu,
                                               bias=e_neg[:, par, k:k + 1], scale=e_rs[:, par, k:k + 1])
                        ins.then_inc(S["e1_relu"], 1)

            edges1(0)
            with act.Fori(1, EG // 2) as i:
                edges1(i)

            def edge2(e, par):
                for h in range(2):
                    act.wait_ge(S["e2_T"], 2 * e + h + 1)
                    wait(act, S["e2_scan"], 2 * e + h - 3)
                    A.activation(ehT[:, par, h * HC:(h + 1) * HC], Te[h][:, :], ACT.Relu,
                                 bias=b1c[:, :]).then_inc(S["e2_relu"], 1)

            def step2(j, epar):
                edge2(j, epar)
                back("d2", 2 * j + 1, 1)
                back("d2", 2 * j + 2, 0)

            act.wait_ge(S["d1_M"], 2 * NG)
            act.wait_ge(S["e1_T"], 2 * EG)
            back("d2", 0, 0)
            step2(0, 0)
            step2(1, 1)
            with act.Fori(1, (EG - 2) // 2) as i:
                step2(2 * i, 0)
                step2(2 * i + 1, 1)
            edge2(EG - 2, 0)
            edge2(EG - 1, 1)

        @block.tensor
        def _(pe):
            T = nc.tensor

            def turn(t, par, h, bank):
                for k in range(HT):
                    ins = T.transpose(bank[:, k * P:(k + 1) * P], t[:, par, HT * h + k, :], ident[:, :])
                return ins

            def dense_T(L, g, par, i):
                for h in range(2):
                    if L == "d1":
                        pe.wait_ge(S["d1_relu"], 2 * g + h + 1)
                    else:
                        pe.wait_ge(S["d2_p"][par], 16 * (i + 1))
                    wait(pe, S[L + "_hT"], 2 * g + h - 1)
                    turn(dh, par, h, Td[h]).then_inc(S[L + "_T"], 1)

            def dense_M(L, g, par, root):
                for h in range(2):
                    pe.wait_ge(S[L + "_hT"], 2 * g + h + 1)
                    wait(pe, S[L + "_evac"], 2 * g + h - 1)
                    for k in range(HT):
                        ins = T.matmul(Md[h][:, k * C:(k + 1) * C], dT[:, par, (HT * h + k) * P:(HT * h + k + 1) * P],
                                       root[:, :], start=True, stop=True)
                    ins.then_inc(S[L + "_M"], 1)

            def edge_T(L, e, par, i):
                for h in range(2):
                    if L == "e1":
                        pe.wait_ge(S["e1_relu"], 2 * e + h + 1)
                        wait(pe, S["e1_scan"], 2 * e + h - 1)
                        turn(eh, par, h, Te[h]).then_inc(S["e1_T"], 1)
                    else:
                        pe.wait_ge(S["e2_in"][par], 16 * K * (i + 1))
                        wait(pe, S["e2_relu"], 2 * e + h - 1)
                        turn(eg, par, h, Te[h]).then_inc(S["e2_T"], 1)

            def edge_rels(e):
                return [pe.value_load(rels[0:1, bass.ds(2 * e + h, 1)], min_val=0, max_val=16 ** HT - 1)
                        for h in range(2)]

            def edge_M(L, e, par, w, rel):
                for h in range(2):
                    pe.wait_ge(S[L + "_scan"], 2 * e + h + 1)
                    wait(pe, S[L + "_evac"], 2 * e + h - 1)
                    for k in range(HT):
                        col = ((rel[h] >> (4 * k)) & 15) * C + w
                        ins = T.matmul(Me[h][:, k * C:(k + 1) * C], sums[:, par, (HT * h + k) * P:(HT * h + k + 1) * P],
                                       w_all[:, bass.ds(col, C)], start=True, stop=True)
                    ins.then_inc(S[L + "_M"], 1)

            pe.wait_ge(S["made"], 1)
            pe.wait_ge(S["rec_ready"], 1)
            T.matmul(Me[0][:, 0:R], tri[:, :], n_f, start=True, stop=True)
            T.matmul(Me[0][:, R:2 * R], ones[:, :], n_f, start=True, stop=True).then_inc(S["offs"], 1)

            pe.wait_ge(S["consts_in"], 96)

            def pair1(i):
                dense_M("d1", 2 * i, 0, r1)
                dense_T("d1", 2 * i + 1, 1, i)
                dense_M("d1", 2 * i + 1, 1, r1)
                dense_T("d1", 2 * i + 2, 0, i)

            dense_T("d1", 0, 0, 0)
            pair1(0)
            with pe.Fori(1, NG // 2) as i:
                pair1(i)
            dense_M("d1", NG - 1, 0, r1)

            pe.wait_ge(S["d1_hT"], 2 * NG)
            pe.wait_ge(S["tops_in"], 1)
            for h in range(2):
                T.transpose(Td[0][0:1, h * HR:(h + 1) * HR], begun[0:HR, h, P - 1:P], ident[0:HR, 0:HR])
            for h in range(2):
                ins = T.transpose(Td[1][0:1, h * HR:(h + 1) * HR], rel_rf[0:HR, h:h + 1], ident[0:HR, 0:HR])
            ins.then_inc(S["tops_t"], 1)
            pe.wait_ge(S["tops_in"], 2)
            for h in range(2):
                ins = T.transpose(Te[0][0:HR, h:h + 1], top_sum[0:1, h * HR:(h + 1) * HR], ident[0:1, 0:1])
            ins.then_inc(S["tops_b"], 1)
            pe.wait_ge(S["tops_in"], 3)
            for h in range(2):
                for bank, a in ((Td[0], cur[0:HR, h, :, 0]), (Td[1], aim[0:HR, h, :]), (Te[1], recip[0:HR, h, :])):
                    ins = T.transpose(bank[:, h * HR:(h + 1) * HR], a, ident[0:HR, 0:HR])
            ins.then_inc(S["metaT"], 1)
            pe.wait_ge(S["meta"], 2)

            def edges1(i):
                for par in range(2):
                    rel = edge_rels(2 * i + par)
                    edge_T("e1", 2 * i + par, par, i)
                    edge_M("e1", 2 * i + par, par, 0, rel)

            edges1(0)
            with pe.Fori(1, EG // 2) as i:
                edges1(i)

            def step2(j, i, epar):
                rel = edge_rels(j)
                edge_T("e2", j, epar, i)
                dense_M("d2", 2 * j, 0, r2)
                dense_T("d2", 2 * j + 1, 1, j)
                edge_M("e2", j, epar, R * C, rel)
                dense_M("d2", 2 * j + 1, 1, r2)
                dense_T("d2", 2 * j + 2, 0, j + 1)

            dense_T("d2", 0, 0, 0)
            step2(0, 0, 0)
            step2(1, 0, 1)
            with pe.Fori(1, (EG - 2) // 2) as i:
                step2(2 * i, i, 0)
                step2(2 * i + 1, i, 1)
            dense_M("d2", NG - 1, 0, r2)
            for par in range(2):
                rel = edge_rels(EG - 2 + par)
                edge_T("e2", EG - 2 + par, par, EG // 2 - 1)
                edge_M("e2", EG - 2 + par, par, R * C, rel)


_NAMES = {"x": "x", "src": "src", "dst": "dst", "attr": "edge_attr_42",
          "w_rel1": "L0_gnn_w_rel1", "root1": "L0_gnn_root1", "b1": "L0_gnn_b1",
          "w_rel2": "L0_gnn_w_rel2", "root2": "L0_gnn_root2", "b2": "L0_gnn_b2"}


def kernel(**inputs):
    import numpy as np
    import concourse.bacc as bacc
    from concourse.bass_utils import run_bass_kernel_spmd

    nc = bacc.Bacc("TRN2", target_bir_lowering=False, num_devices=1)
    arrays, args = {}, []
    for short, name in _NAMES.items():
        a = np.ascontiguousarray(inputs[name])
        if short in ("src", "dst"):
            a = a.reshape(-1, 1)
        arrays[f"in_{short}"] = a
        args.append(nc.dram_tensor(f"in_{short}", a.shape, mybir.dt.from_np(a.dtype), kind="ExternalInput").ap())
    args.append(nc.dram_tensor("out_rows", (N + SPARE, C), F32, kind="ExternalOutput").ap())
    build(nc, *args)
    r = run_bass_kernel_spmd(nc, [arrays], core_ids=[0])
    return r.results[0]["out_rows"][:N]
```

```python
import concourse.bass as bass
from concourse import mybir
from contextlib import ExitStack, nullcontext

F32, I32, U8 = mybir.dt.float32, mybir.dt.int32, mybir.dt.uint8
ALU, ACT, AX = mybir.AluOpType, mybir.ActivationFunctionType, mybir.AxisListType

P = 128
N, C, E, R = 50000, 128, 25000, 10
ATTR, REL0 = 42, 16
EPS = 1e-5
K = 8
HT = K // 2
HC = HT * C
GROUP = K * P
J = -(-E // P)
TAIL_P, TAIL_J = E // J, E % J
JH = J // 2
PIECES = ((0, J // 14), (J // 14, J))
NG = -(-N // GROUP)
OVER = (NG * GROUP - N) // K
USED = (E + R * (P - 1)) // P
TILES = -(-USED // K) * K
EG = TILES // K
LAST = USED - (EG - 1) * K
SLOTS = TILES * P
HR = TILES // 2
SPARE = 2 * GROUP
KEY = 1 << 16
PADKEY = R * KEY
TROWS = -(-(SLOTS + 2) // P) * P
SKIP = 1 << 20
LATE = 3
assert J % 2 == 0 and JH < TAIL_J and HR <= P and (NG * GROUP - N) % K == 0
assert NG % 4 == 1 and EG % 2 == 0 and 2 * (EG - 2) == NG - 1


def wait(eng, sem, value):
    if not (isinstance(value, int) and value <= 0):
        eng.wait_ge(sem, value)


def alone(eng, ticks):
    eng.sem_inc(ticks, 1)


class Own:

    def __init__(self, eng, sem):
        self.eng, self.sem, self.base, self.n = eng, sem, 0, 0

    def done(self, ins):
        ins.then_inc(self.sem, 1)
        self.n += 1
        self.eng.wait_ge(self.sem, self.base + self.n)

    def mark(self, ins):
        ins.then_inc(self.sem, 1)
        self.n += 1
        return self.n

    def until(self, n):
        self.eng.wait_ge(self.sem, self.base + n)

    def enter(self, i, per):
        self.start = self.base + self.n if self.n or isinstance(self.base, int) else self.start
        self.base, self.per, self.n = self.start + i * per, per, 0

    def leave(self, times):
        assert self.n == self.per, (self.n, self.per)
        self.base, self.n = self.start + times * self.per, 0


def build(nc, x, src, dst, attr, w_rel1, root1, b1, w_rel2, root2, b2, out):
    ctx = ExitStack()
    with ctx:
        def sb(name, shape, dt=F32):
            return ctx.enter_context(nc.sbuf_tensor(name, shape, dt))

        def sem(name):
            return ctx.enter_context(nc.semaphore(name))

        def dram(name, shape, dt=F32):
            return nc.dram_tensor(name, shape, dt, kind="Internal").ap()

        pre1 = dram("pre1", (N + SPARE, C))
        table = dram("slot_table", (TROWS, 2))
        mask_d = dram("mask_d", (TILES, P), U8)

        w_all = sb("w_all", [P, (R + 16) * C])
        w1, w2 = w_all[:, 0:R * C], w_all[:, R * C:2 * R * C]
        r1, r2, b2b, ident = (w_all[:, (2 * R + n) * C:(2 * R + n + 1) * C] for n in range(4))
        b1c = sb("b1c", [P, 1])
        eps = sb("eps", [P, 1])

        msg2 = sb("msg2", [P, TILES, C])
        scratch = msg2[:, :, :].rearrange("p t c -> p (t c)")
        at = [0]

        def carve(n, dt=F32):
            at[0] += n
            assert at[0] <= TILES * C
            v = scratch[:, at[0] - n:at[0]]
            return v if dt is F32 else v.bitcast(dt)

        attr_s = carve(J * ATTR).rearrange("p (j a) -> p j a", a=ATTR)
        cand = carve(J * R).rearrange("p (j r) -> p j r", r=R)
        hot = carve(R * J).rearrange("p (r j) -> p r j", r=R)
        goes_on = carve(R * J).rearrange("p (r j) -> p r j", r=R)
        rank = carve(R * J).rearrange("p (r j) -> p r j", r=R)
        src_i0, dst_i0 = carve(J, I32), carve(J, I32)
        e_no, best, rel, void, past = (carve(J) for _ in range(5))
        row_f, row_i = carve(J), carve(J, I32)
        rec = carve(J * 2).rearrange("p (j c) -> p j c", c=2)
        r_no = carve(R)
        both = carve(2 * R)
        tri, ones = carve(P), carve(P)
        n_i, n_f, n_sum, shift = carve(R, I32), carve(R), carve(R), carve(R)
        fill = carve(TROWS // P * 2).rearrange("p (j c) -> p j c", c=2)
        zeros = carve(SPARE // P * C)

        def halves(dt=F32):
            return carve(2 * P, dt).rearrange("p (h i) -> p h i", h=2)

        s_no, s_i = halves(), halves(I32)
        at[0] = 0
        cur = carve(2 * P * 2).rearrange("p (h i c) -> p h i c", h=2, c=2)
        prev = carve(2 * P * 2).rearrange("p (h i c) -> p h i c", h=2, c=2)
        nxt = carve(2 * P * 2).rearrange("p (h i c) -> p h i c", h=2, c=2)

        same, last, first, begun, count, node, spare, aim = (halves() for _ in range(8))
        key_i, node_i = halves(I32), halves(I32)
        carry = carve(2)
        rel_ri, rel_rf = carve(2, I32), carve(2)
        tops, top_sum = carve(TILES + 1), carve(TILES + 1)
        rel_c, power, flag = carve(TILES), carve(TILES), carve(TILES)
        flag_f, packed, packed_f = carve(EG), carve(TILES), carve(TILES // HT)
        shift4, full, full_f, full_n = carve(TILES), carve(LAST), carve(1), carve(1)
        rec_first = carve(2 * K * 2).rearrange("p (k c) -> p k c", c=2)
        rec_last = carve(K * 2).rearrange("p (k c) -> p k c", c=2)
        key_first, key_last = rec_first[:, :, 1], rec_last[:, :, 1]
        low_i, low, low_rel_i, low_rel = carve(2 * K, I32), carve(2 * K), carve(2 * K, I32), carve(2 * K)
        high_i, high, open_end, meet = carve(K, I32), carve(K), carve(K), carve(1)
        top = carve(1)
        below, over = (carve(2 * K * K).rearrange("p (t u) -> p t u", t=K) for _ in range(2))

        same_b = carve(2 * P // 4, U8).rearrange("p (h i) -> p h i", h=2)
        src_all, aim_all = sb("src_all", [P, TILES + 2 * K], I32), sb("aim_all", [P, TILES], I32)
        rc_all = sb("rc_all", [P, TILES])
        rels = sb("rels", [1, TILES // HT], I32)
        starts = sb("starts", [1, EG + 3], I32)

        mask = sb("mask", [P, EG, GROUP], U8)

        g_idx, s_idx = sb("g_idx", [P, 2, K], I32), sb("s_idx", [P, 2, K], I32)
        eg, eh = sb("eg", [P, 2, K, C]), sb("eh", [P, 2, K, C])
        ehT = eh[:, :, :, :].rearrange("p a k c -> p a (k c)")
        sums = sb("sums", [P, 2, GROUP])
        msg = sb("msg", [P, 2, K, C])
        dx = sb("dx", [P, K, C])[:, :, :]
        x_even = [dx, msg[:, 1]]
        x_ring = [dx, msg[:, 0], eg[:, 0], eg[:, 1]]
        dh = sb("dh", [P, 2, K, C])
        dT = sb("dT", [P, 2, GROUP])
        do = sb("do", [P, 2, K, C])
        d_st = e_st = sb("d_st", [P, K, 6])
        d_mv, e_mv = sb("d_mv", [P, 2, K, 2]), sb("e_mv", [P, 2, K, 2])
        d_neg, d_sd, d_rs = sb("d_neg", [P, 2, K]), sb("d_sd", [P, 2, K]), sb("d_rs", [P, 2, K])
        e_neg, e_sd, e_rs = sb("e_neg", [P, 2, K]), sb("e_sd", [P, 2, K]), sb("e_rs", [P, 2, K])

        ps = [ctx.enter_context(nc.psum_tensor(f"bank{n}", [P, HC], F32)) for n in range(8)]
        Td, Te, Md, Me = ps[0:2], ps[2:4], ps[4:6], ps[6:8]

        S = {}
        for name in ("rec_out attr_in attr_in2 ids_in consts_in made pads_set filled spare_zero rec_ready offs sorted "
                     "last_in p1_done cur_in m_in keys_in tops_t tops_in tops_b src_T metaT mask_out meta x_kept "
                     "d1_mean d1_neg d1_std d1_relu d1_T d1_hT d1_M d1_evac "
                     "next e1_mean e1_std e1_par e1_relu e1_T e1_scan e1_M e1_evac "
                     "d2_T d2_hT d2_M d2_evac e2_relu e2_T e2_scan e2_M e2_evac staged "
                     "dve_own pool_own dve_ticks pool_ticks").split():
            S[name] = sem(name)
        S["d1_in"] = [sem(f"d1_in{n}") for n in range(4)]
        for name in "d1_stored e1_in mask_in e1_add d2_p d2_x d2_stored e2_in e2_add".split():
            S[name] = [sem(f"{name}{n}") for n in range(2)]

        block = ctx.enter_context(nc.Block())

        def rows(a, g):
            base = g * GROUP if not isinstance(g, int) else min(g * GROUP, N - GROUP)
            return a[bass.ds(base, GROUP), :].rearrange("(p k) c -> p (k c)", k=K)

        def flat(t, par):
            return t[:, par, :, :].rearrange("p k c -> p (k c)")

        def kept(j):
            return msg2[:, bass.ds(j * K, K), :]

        def shifted(by):
            return [table[by + h * HR * P:by + (h + 1) * HR * P, :].rearrange("(t i) c -> t (i c)", i=P)
                    for h in range(2)]

        @block.sync
        def _(sp):
            whole = TAIL_P // 16 * 16

            def load_edges(a, t, j0, j1, done):
                v = a[0:TAIL_P * J].rearrange("(p j) a -> p j a", j=J)[:, j0:j1].rearrange("p j a -> p (j a)")
                for p in (slice(0, whole), slice(whole, TAIL_P)):
                    sp.dma_start(t[p, j0:j1].rearrange("p j a -> p (j a)"), v[p]).then_inc(S[done], 16)
                tail = a[TAIL_P * J + j0:min(TAIL_P * J + j1, E)].rearrange("(p j) a -> p (j a)", p=1)
                sp.dma_start(t[TAIL_P:TAIL_P + 1, j0:min(j1, TAIL_J)].rearrange("p j a -> p (j a)"),
                             tail).then_inc(S[done], 16)

            load_edges(attr, attr_s, 0, JH, "attr_in")
            sp.wait_ge(S["pads_set"], 1)
            load_edges(attr, attr_s, JH, J, "attr_in2")
            load_edges(src, src_i0.unsqueeze(2), 0, J, "ids_in")
            load_edges(dst, dst_i0.unsqueeze(2), 0, J, "ids_in")
            sp.wait_ge(S["pads_set"], 3)
            sp.dma_start(table.rearrange("(p j) c -> p (j c)", p=P),
                         fill.rearrange("p j c -> p (j c)")).then_inc(S["filled"], 16)
            for t in (pre1, out):
                sp.dma_start(t[N:N + SPARE, :].rearrange("(p k) c -> p (k c)", p=P),
                             zeros).then_inc(S["spare_zero"], 16)
            for t, a in ((w1, w_rel1), (w2, w_rel2)):
                sp.dma_start(t.rearrange("c (r o) -> c r o", r=R),
                             a.rearrange("r c o -> c r o")).then_inc(S["consts_in"], 16)
            for t, a in ((r1, root1), (r2, root2), (b1c, b1.unsqueeze(1)),
                         (b2b, b2.partition_broadcast(P))):
                sp.dma_start(t[:, :], a).then_inc(S["consts_in"], 16)

            def load1(g, q):
                wait(sp, S["d1_relu"], 2 * g - 6)
                sp.dma_start(x_ring[q].rearrange("p k c -> p (k c)"), rows(x, g)).then_inc(S["d1_in"][q], 16)

            def own_rows(g):
                return slice(OVER if isinstance(g, int) and g == NG - 1 else 0, P)

            def store1(g, par):
                sp.wait_ge(S["d1_evac"], 2 * g + 2)
                sp.dma_start(rows(pre1, g)[own_rows(g)],
                             flat(do, par)[own_rows(g)]).then_inc(S["d1_stored"][par], 16)

            def quad1(i, more=4):
                for q in range(4):
                    if q < more:
                        load1(4 * i + 4 + q, q)
                    store1(4 * i + q, q % 2)

            for q in range(4):
                load1(q, q)
            quad1(0)
            with sp.Fori(1, NG // 4 - 1) as i:
                quad1(i)
            quad1(NG // 4 - 1, more=1)

            sp.wait_ge(S["rec_out"], 16 * J)
            for t, by in ((cur, 1), (prev, 0), (nxt, 2)):
                for h, v in enumerate(shifted(by)):
                    sp.dma_start(t[0:HR, h].rearrange("p i c -> p (i c)"),
                                 v).then_inc(S["cur_in" if by == 1 else "m_in"], 16)
            store1(NG - 1, 0)
            tile_recs = table[1:1 + SLOTS, :].rearrange("(t i) c -> t i c", i=P)
            for t, i, before in ((rec_first[0:EG, K:2 * K], 0, 0), (rec_first[1:EG, 0:K], 0, 1),
                                 (rec_last[0:EG], P - 1, 0)):
                v = tile_recs[0:(EG - before) * K, i, :].rearrange("(e k) c -> e k c", k=K)
                sp.dma_start(t, v).then_inc(S["keys_in"], 16)
            sp.wait_ge(S["meta"], 1)
            for h in range(2):
                sp.dma_start(mask_d[h * HR:(h + 1) * HR, :], same_b[0:HR, h, :]).then_inc(S["mask_out"], 16)
            sp.wait_ge(S["mask_out"], 32)

            def masks1(i):
                for par in range(2):
                    e = 2 * i + par
                    wait(sp, S["e1_scan"], 2 * e - 2)
                    v = mask_d[bass.ds(e * K, K), :].rearrange("t i -> (t i)").partition_broadcast(P)
                    sp.dma_start(mask[:, bass.ds(e, 1), :].rearrange("p e i -> p (e i)"),
                                 v).then_inc(S["mask_in"][par], 16)

            def load_x(j, epar):
                sp.dma_start(x_even[epar].rearrange("p k c -> p (k c)"),
                             rows(x, 2 * j)).then_inc(S["d2_x"][epar], 16)

            def keep_x(j, g):
                sp.dma_start(kept(j).rearrange("p k c -> p (k c)"), rows(x, g)).then_inc(S["x_kept"], 16)

            masks1(0)
            sp.wait_ge(S["meta"], 3)
            sp.wait_ge(S["spare_zero"], 32)
            with sp.Fori(1, EG // 2) as i:
                masks1(i)
                keep_x(2 * i - 2, 4 * i - 3)
                keep_x(2 * i - 1, 4 * i - 1)
            keep_x(EG - 1, NG - 1)
            load_x(0, 0)

            sp.wait_ge(S["p1_done"], 1)

            def load_p(g, par):
                wait(sp, S["d2_T"], 2 * g - 2)
                sp.dma_start(flat(dh, par), rows(pre1, g)).then_inc(S["d2_p"][par], 16)

            def store2(g, par):
                sp.wait_ge(S["d2_evac"], 2 * g + 2)
                sp.dma_start(rows(out, g)[own_rows(g)],
                             flat(do, par)[own_rows(g)]).then_inc(S["d2_stored"][par], 16)

            def pair2(j, xpar, more_p=True, more_x=True):
                load_p(2 * j + 2, 0)
                store2(2 * j, 0)
                if more_x:
                    load_x(j + 2, xpar)
                if more_p:
                    load_p(2 * j + 3, 1)
                store2(2 * j + 1, 1)

            for par in range(2):
                load_p(par, par)
            sp.wait_ge(S["e1_evac"], 2 * EG)
            load_x(1, 1)
            pair2(0, 0)
            pair2(1, 1)
            with sp.Fori(1, NG // 4 - 1) as i:
                pair2(2 * i, 0)
                pair2(2 * i + 1, 1)
            pair2(NG // 2 - 2, 0, more_x=False)
            pair2(NG // 2 - 1, 1, more_x=False, more_p=False)
            store2(NG - 1, 0)
            sp.wait_ge(S["d2_stored"][1], 16 * (NG // 2))
            sp.wait_ge(S["d2_stored"][0], 16 * (NG // 2 + 1))

        @block.gpsimd
        def _(pool):
            own = Own(pool, S["pool_own"])
            pool.memset(ident[:, :], 0.0)
            own.done(pool.memset(ones, 1.0))
            pool.affine_select(out=ident[:, :], in_=ident[:, :], compare_op=ALU.not_equal, fill=1.0,
                               base=0, pattern=[[-1, P]], channel_multiplier=1)
            pool.affine_select(out=tri, in_=ones, compare_op=ALU.is_gt, fill=0.0,
                               base=0, pattern=[[1, P]], channel_multiplier=-1)
            pool.iota(e_no, pattern=[[1, J]], base=0, channel_multiplier=J,
                      allow_small_or_imprecise_dtypes=True)
            pool.iota(r_no, pattern=[[1, R]], base=0, channel_multiplier=0,
                      allow_small_or_imprecise_dtypes=True)
            pool.iota(s_no[0:HR], pattern=[[HR * P, 2], [1, P]], base=0, channel_multiplier=P,
                      allow_small_or_imprecise_dtypes=True)
            pool.iota(s_i[0:HR], pattern=[[HR * P, 2], [1, P]], base=0,
                      channel_multiplier=P).then_inc(S["made"], 1)

            pool.wait_ge(S["filled"], 16)
            for n, (j0, j1) in enumerate(PIECES):
                pool.wait_ge(S["sorted"], n + 1)
                for j in range(j0, j1):
                    pool.indirect_dma_start(
                        table, bass.IndirectOffsetOnAxis(ap=row_i[:, j:j + 1], axis=0), rec[:, j, :], None,
                        bounds_check=TROWS - 1, oob_is_err=False).then_inc(S["rec_out"], 16)

            def last_tiles():
                return pool.value_load(starts[0:1, EG:EG + 1], min_val=0, max_val=(1 << LAST) - 1)

            def group(e):
                return pool.If(last_tiles()) if isinstance(e, int) and e == EG - 1 else nullcontext()

            def each_tile(e, do):
                if not isinstance(e, int) or e < EG - 1:
                    for k in range(K):
                        do(k)
                    return
                full = last_tiles()
                for k in range(LAST):
                    with pool.If(full & (1 << k)):
                        do(k)

            def all_in(done, said=None):
                tiles = pool.value_load(starts[0:1, EG + 1:EG + 2], min_val=0, max_val=LAST)
                pool.wait_ge(done[1], tiles * 16 + 16 * K * (EG // 2 - 1))
                alone(pool, said or S["pool_ticks"])

            def gather(table_, e, i, par, before, done):
                def fetch(k):
                    pool.indirect_dma_start(
                        eg[:, par, k, :], None, table_,
                        bass.IndirectOffsetOnAxis(ap=g_idx[:, par, k:k + 1], axis=0)
                    ).then_inc(S[done][par], 16)

                with group(e):
                    pool.wait_ge(S["next"], e + before + 1)
                    alone(pool, S["pool_ticks"])
                    each_tile(e, fetch)

            def scatter_add(table_, e, i, par, done, ready, count):
                def add(k):
                    pool.indirect_dma_start(
                        table_, bass.IndirectOffsetOnAxis(ap=s_idx[:, par, k:k + 1], axis=0),
                        msg[:, par, k, :], None, compute_op=ALU.add).then_inc(S[done][par], 16)

                def all_earlier(k):
                    wait(pool, S[done][par], 16 * (K * i + k))
                    wait(pool, S[done][1 - par], 16 * K * (i + par))
                    alone(pool, S["pool_ticks"])

                def add_after(k):
                    with pool.If(bits & (1 << k)):
                        all_earlier(k)
                    add(k)

                with group(e):
                    bits = pool.value_load(starts[0:1, bass.ds(e, 1)], min_val=0, max_val=(1 << K) - 1)
                    pool.wait_ge(S[ready], count)
                    alone(pool, S["pool_ticks"])
                    with pool.If(bits):
                        each_tile(e, add_after)
                    with pool.Else():
                        each_tile(e, add)

            def pair1(i, more=True):
                for par in range(2):
                    if more:
                        gather(x, 2 * i + par + 2, i, par, 0, "e1_in")
                    if isinstance(i, int) and i == 0 and par == 0:
                        pool.wait_ge(S["meta"], 2)
                        pool.wait_ge(S["spare_zero"], 32)
                        pool.wait_ge(S["d1_stored"][0], 16 * (NG // 2 + 1))
                        pool.wait_ge(S["d1_stored"][1], 16 * (NG // 2))
                    e = 2 * i + par
                    scatter_add(pre1, e, i, par, "e1_add", "e1_evac", 2 * e + 2)
                    if isinstance(e, int) and e == EG - 3:
                        all_in(S["e1_in"], S["last_in"])

            for par in range(2):
                gather(x, par, 0, par, 0, "e1_in")
            pair1(0)
            with pool.Fori(1, EG // 2 - 2) as i:
                pair1(i)
            pair1(EG // 2 - 2)
            pair1(EG // 2 - 1, more=False)

            pool.wait_ge(S["e1_add"][0], 16 * K * EG // 2)
            all_in(S["e1_add"], S["p1_done"])

            def gathers2(i):
                for par in range(2):
                    gather(pre1, 2 * i + par, i, par, EG, "e2_in")

            gathers2(0)
            with pool.Fori(1, EG // 2 - 1) as i:
                gathers2(i)
            gathers2(EG // 2 - 1)
            all_in(S["e2_in"], S["last_in"])

            def stored2(groups):
                pool.wait_ge(S["d2_stored"][0], 16 * ((groups + 1) // 2))
                pool.wait_ge(S["d2_stored"][1], 16 * (groups // 2))
                alone(pool, S["pool_ticks"])

            def adds2(i):
                for par in range(2):
                    e = 2 * i + par
                    scatter_add(out, e, i, par, "e2_add", "staged", e + 1)
                    if isinstance(e, int) and e == 0:
                        stored2(NG)

            stored2(NG - LATE)
            with pool.If(pool.value_load(starts[0:1, EG + 2:EG + 3], min_val=0, max_val=1)):
                stored2(NG)
            adds2(0)
            with pool.Fori(1, EG // 2 - 1) as i:
                adds2(i)
            adds2(EG // 2 - 1)
            pool.wait_ge(S["e2_add"][0], 16 * K * EG // 2)
            all_in(S["e2_add"])

        @block.vector
        def _(dve):
            own = Own(dve, S["dve_own"])
            V = nc.vector
            q = TAIL_P // 32 * 32
            V.memset(attr_s[q:P, TAIL_J:J, REL0:REL0 + R], 0.0)
            V.memset(src_i0[q:P, TAIL_J:J], 0)
            V.memset(dst_i0[q:P, TAIL_J:J], 0)
            V.memset(eps[:, :], EPS).then_inc(S["pads_set"], 1)
            V.memset(fill[:, :, 0], 0.0)
            V.memset(fill[:, :, 1], float(PADKEY)).then_inc(S["pads_set"], 1)
            V.memset(zeros, 0.0).then_inc(S["pads_set"], 1)
            own.done(V.memset(goes_on, 1.0))
            own.done(V.memset(goes_on[:, :, 0], 0.0))

            dve.wait_ge(S["made"], 1)
            own.done(V.tensor_scalar(void, e_no, float(E), None, ALU.is_ge))
            V.tensor_scalar(past, void, float(2 * R), float(R), ALU.mult, ALU.add)
            for h, arrived in enumerate(("attr_in", "attr_in2")):
                j = slice(h * JH, (h + 1) * JH)
                dve.wait_ge(S[arrived], 48)
                scores = attr_s[:, j, REL0:REL0 + R]
                own.done(V.tensor_reduce(best[:, j], scores, axis=AX.X, op=ALU.max))
                own.done(V.tensor_tensor(cand[:, j], scores, best[:, j].unsqueeze(2).to_broadcast([P, JH, R]),
                                         ALU.is_equal))
                own.done(V.scalar_tensor_tensor(cand[:, j], cand[:, j], -float(R),
                                                r_no.unsqueeze(1).to_broadcast([P, JH, R]), ALU.mult, ALU.add))
                own.done(V.tensor_reduce(rel[:, j], cand[:, j], axis=AX.X, op=ALU.min))
                own.done(V.tensor_tensor(rel[:, j], rel[:, j], past[:, j], ALU.add))
                for r in range(R):
                    one = V.tensor_scalar(hot[:, r, j], rel[:, j], float(r), None, ALU.is_equal)
            own.done(one)
            own.done(V.tensor_tensor_scan(rank.rearrange("p r j -> p (r j)"),
                                          goes_on.rearrange("p r j -> p (r j)"),
                                          hot.rearrange("p r j -> p (r j)"), 0.0, ALU.mult, ALU.add))
            V.tensor_copy(n_f, rank[:, :, J - 1]).then_inc(S["rec_ready"], 1)
            dve.wait_ge(S["ids_in"], 96)
            V.tensor_copy(rec[:, :, 0], src_i0)
            own.done(V.tensor_copy(row_f, dst_i0))
            own.done(V.scalar_tensor_tensor(rec[:, :, 1], rel, float(KEY), row_f, ALU.mult, ALU.add))
            dve.wait_ge(S["offs"], 1)
            own.done(V.tensor_copy(both, Me[0][:, 0:2 * R]))
            own.done(V.tensor_scalar(n_i, both[:, R:2 * R], float(P - 1), None, ALU.add))
            own.done(V.tensor_scalar(n_i, n_i, 7, None, ALU.logical_shift_right))
            own.done(V.tensor_copy(n_f, n_i))
            own.done(V.tensor_tensor_scan(n_sum, ones[:, 0:R], n_f, 0.0, ALU.mult, ALU.add))
            own.done(V.tensor_tensor(n_sum, n_sum, n_f, ALU.subtract))
            own.done(V.scalar_tensor_tensor(shift, n_sum, float(P), both[:, 0:R], ALU.mult, ALU.add))
            for j0, j1 in PIECES:
                j = slice(j0, j1)
                for r in range(R):
                    one = V.scalar_tensor_tensor(rank[:, r, j], rank[:, r, j], shift[:, r:r + 1], hot[:, r, j],
                                                 ALU.add, ALU.mult)
                own.done(one)
                own.done(V.tensor_reduce(row_f[:, j], rank[:, :, j].rearrange("p r j -> p j r"), axis=AX.X,
                                         op=ALU.add))
                own.done(V.scalar_tensor_tensor(row_f[:, j], void[:, j], float(SKIP), row_f[:, j],
                                                ALU.mult, ALU.add))
                V.tensor_copy(row_i[:, j], row_f[:, j]).then_inc(S["sorted"], 1)

            def stats(t, st):
                for k in range(K):
                    ins = V.bn_stats(st[:, k, :], t[:, k, :])
                return ins

            def moments(st, mv):
                for k in range(K):
                    ins = V.bn_aggr(mv[:, k, :], st[:, k, :])
                return ins

            def back1(g, par, h):
                dve.wait_ge(S["d1_M"], 2 * g + h + 1)
                rs = d_rs[:, par, HT * h:HT * h + HT].unsqueeze(2).to_broadcast([P, HT, C])
                V.tensor_tensor(do[:, par, HT * h:HT * h + HT, :], Md[h][:, :].rearrange("p (k c) -> p k c", c=C),
                                rs, ALU.mult).then_inc(S["d1_evac"], 1)

            def step1(i, q, ahead=2):
                g, par, q2 = 4 * i + q, q % 2, (q + 2) % 4
                if ahead == 2:
                    dve.wait_ge(S["d1_in"][q2], 16 * (i + 1 + (q + 2) // 4))
                    dve.wait_ge(S["d1_mean"], g + 2)
                    seen = own.mark(stats(x_ring[q2], d_st))
                if ahead:
                    dve.wait_ge(S["d1_std"], g + 2)
                    wait(dve, S["d1_evac"], 2 * g)
                    own.mark(V.reciprocal(d_rs[:, 1 - par, :], d_sd[:, 1 - par, :]))
                if ahead == 2:
                    own.until(seen)
                    alone(dve, S["dve_ticks"])
                    moments(d_st, d_mv[:, par]).then_inc(S["d1_mean"], 1)
                wait(dve, S["d1_stored"][par], 16 * (2 * i + q // 2))
                back1(g, par, 0)
                back1(g, par, 1)

            for g in range(2):
                dve.wait_ge(S["d1_in"][g], 16)
                wait(dve, S["d1_mean"], g)
                own.done(stats(x_ring[g], d_st))
                moments(d_st, d_mv[:, g]).then_inc(S["d1_mean"], 1)
            dve.wait_ge(S["d1_std"], 1)
            own.done(V.reciprocal(d_rs[:, 0, :], d_sd[:, 0, :]))
            for q in range(4):
                step1(0, q)
            with dve.Fori(1, NG // 4 - 1) as i:
                own.enter(i - 1, 8)
                for q in range(4):
                    step1(i, q)
            own.leave(NG // 4 - 2)
            for q in range(4):
                step1(NG // 4 - 1, q, ahead=2 if q < 3 else 1)
            step1(NG // 4, 0, ahead=0)

            def first_indices():
                for par in range(2):
                    V.tensor_copy(g_idx[:, par, :], src_all[:, par * K:par * K + K]).then_inc(S["next"], 1)

            def measure(e, i, par):
                if isinstance(e, int) and e == EG - 1:
                    dve.wait_ge(S["last_in"], 1)
                else:
                    dve.wait_ge(S["e1_in"][par], 16 * K * (i + 1))
                wait(dve, S["e1_relu"], 2 * e - 2)
                own.done(stats(eg[:, par], e_st))
                alone(dve, S["dve_ticks"])
                moments(e_st, e_mv[:, par]).then_inc(S["e1_mean"], 1)

            def scales(e, par):
                dve.wait_ge(S["e1_std"], e + 1)
                own.done(V.reciprocal(e_rs[:, par, :], e_sd[:, par, :]))
                V.scalar_tensor_tensor(e_neg[:, par, :], e_mv[:, par, :, 0], -1.0, e_rs[:, par, :],
                                       ALU.mult, ALU.mult).then_inc(S["e1_par"], 1)

            V.memset(key_first[0:1, 0:K], float(15 * KEY))
            V.memset(flag[0:1, 0:1], 0.0)
            for k in range(K):
                V.memset(power[0:1].rearrange("p (g k) -> p g k", k=K)[:, :, k], float(1 << k))
                V.memset(shift4[0:1].rearrange("p (g k) -> p g k", k=K)[:, :, k], float(16 ** (k % HT)))
            dve.wait_ge(S["src_T"], 1)
            own.done(V.tensor_copy(src_all[:, 0:TILES], Me[1][:, 0:TILES]))
            first_indices()
            V.tensor_copy(src_all[:, TILES:], src_all[:, 0:2 * K])
            dve.wait_ge(S["cur_in"], 32)
            dve.wait_ge(S["m_in"], 64)
            key = cur[0:HR, :, :, 1]
            r = slice(0, HR)
            V.tensor_tensor(same[r], key, prev[r, :, :, 1], ALU.is_equal)
            V.tensor_tensor(last[r], key, nxt[r, :, :, 1], ALU.not_equal)
            V.tensor_copy(key_i[r], key)
            V.tensor_scalar(first[r], key, float(PADKEY), None, ALU.is_lt)
            own.done(V.tensor_scalar(node_i[r], s_i[r], SPARE - 1, None, ALU.bitwise_and))
            V.tensor_copy(same_b[r], same[r]).then_inc(S["meta"], 1)
            V.tensor_tensor(last[r], last[r], first[r], ALU.mult)
            V.tensor_copy(spare[r], node_i[r])
            own.done(V.tensor_scalar(rel_ri[r], key_i[r, :, 0], 16, None, ALU.logical_shift_right))
            V.tensor_scalar(node_i[r], key_i[r], KEY - 1, None, ALU.bitwise_and)
            V.tensor_scalar(spare[r], spare[r], float(N), None, ALU.add)
            V.tensor_copy(rel_rf[r], rel_ri[r])
            own.done(V.tensor_scalar(first[r], same[r], -1.0, 1.0, ALU.mult, ALU.add))
            V.tensor_copy(node[r], node_i[r])
            own.done(V.tensor_tensor(first[r], first[r], s_no[r], ALU.mult))
            g = slice(0, EG)
            dve.wait_ge(S["keys_in"], 48)
            V.tensor_copy(low_i[g], key_first[g])
            V.tensor_scalar(open_end[g], key_last[g], float(PADKEY), None, ALU.is_equal)
            own.done(V.tensor_copy(high_i[g], key_last[g]))
            V.tensor_scalar(low_rel_i[g], low_i[g], 16, None, ALU.logical_shift_right)
            V.tensor_scalar(high_i[g], high_i[g], KEY - 1, None, ALU.bitwise_and)
            own.done(V.tensor_scalar(low_i[g], low_i[g], KEY - 1, None, ALU.bitwise_and))
            V.tensor_copy(low_rel[g], low_rel_i[g])
            V.tensor_copy(low[g], low_i[g])
            own.done(V.tensor_copy(high[g], high_i[g]))
            own.done(V.scalar_tensor_tensor(high[g], open_end[g], float(KEY), high[g], ALU.mult, ALU.add))
            V.tensor_scalar(open_end[g], low_rel[g, K:2 * K], float(R), None, ALU.is_lt)
            own.done(V.tensor_tensor(below[g], low_rel[g].unsqueeze(1).to_broadcast([EG, K, 2 * K]),
                                     low_rel[g, K:2 * K].unsqueeze(2).to_broadcast([EG, K, 2 * K]), ALU.is_lt))
            V.tensor_tensor(over[g], high[g].unsqueeze(2).to_broadcast([EG, K, 2 * K]),
                            low[g].unsqueeze(1).to_broadcast([EG, K, 2 * K]), ALU.is_ge)
            own.done(V.tensor_tensor(below[g], below[g], open_end[g].unsqueeze(2).to_broadcast([EG, K, 2 * K]),
                                     ALU.mult))
            own.done(V.tensor_tensor(over[g], over[g], below[g], ALU.mult))
            V.tensor_reduce(top[0:1], high[0:1], axis=AX.X, op=ALU.max)
            own.done(V.tensor_reduce(meet[g], over[g].rearrange("p t u -> p (t u)"), axis=AX.X, op=ALU.max))
            V.tensor_scalar(starts[0:1, EG + 2:EG + 3], top[0:1], float((NG - LATE) * GROUP), None, ALU.is_ge)
            for h in range(2):
                ins = V.tensor_tensor_scan(begun[r, h], first[r, h], first[r, h], 0.0, ALU.max, ALU.max)
            ins.then_inc(S["tops_in"], 1)
            own.done(V.tensor_tensor(node[r], node[r], spare[r], ALU.subtract))
            own.done(V.tensor_tensor(node[r], node[r], last[r], ALU.mult))
            own.done(V.tensor_tensor(aim[r], node[r], spare[r], ALU.add))
            dve.wait_ge(S["d1_mean"], NG)
            measure(0, 0, 0)
            V.memset(tops[0:1, 0:1], 0.0)
            dve.wait_ge(S["tops_t"], 1)
            V.tensor_copy(tops[0:1, 1:TILES + 1], Td[0][0:1, 0:TILES])
            V.tensor_scalar(full[0:1], Td[1][0:1, (EG - 1) * K:USED], float(R), None, ALU.is_lt)
            own.done(V.tensor_scalar(rel_c[0:1], Td[1][0:1, 0:TILES], float(R - 1), None, ALU.min))
            V.tensor_tensor_scan(top_sum[0:1], tops[0:1], tops[0:1], 0.0, ALU.max,
                                 ALU.max).then_inc(S["tops_in"], 1)
            scales(0, 0)
            V.tensor_reduce(full_n[0:1], full[0:1], axis=AX.X, op=ALU.add)
            own.done(V.tensor_tensor(flag[0:1, 1:TILES], rel_c[0:1, 1:TILES], rel_c[0:1, 0:TILES - 1],
                                     ALU.not_equal))
            V.tensor_copy(starts[0:1, EG + 1:EG + 2], full_n[0:1])
            V.tensor_tensor(full[0:1], full[0:1], power[0:1, 0:LAST], ALU.mult)
            V.tensor_tensor(packed[0:1], rel_c[0:1], shift4[0:1], ALU.mult)
            own.done(V.tensor_tensor(flag[0:1], flag[0:1], power[0:1], ALU.mult))
            V.tensor_reduce(full_f[0:1], full[0:1], axis=AX.X, op=ALU.add)
            V.memset(flag[0:1].rearrange("p (g k) -> p g k", k=K)[:, :, 0], 1.0)
            own.done(V.tensor_reduce(packed_f[0:1], packed[0:1].rearrange("p (g k) -> p g k", k=HT),
                                     axis=AX.X, op=ALU.add))
            V.tensor_copy(starts[0:1, EG:EG + 1], full_f[0:1])
            V.tensor_copy(rels[0:1, :], packed_f[0:1])
            own.done(V.tensor_reduce(flag_f[0:1], flag[0:1].rearrange("p (g k) -> p g k", k=K),
                                     axis=AX.X, op=ALU.add))
            own.done(V.tensor_tensor(flag_f[0:1], flag_f[0:1], Td[1][0:1, TILES:TILES + EG], ALU.mult))
            V.tensor_copy(starts[0:1, 0:EG], flag_f[0:1])
            dve.wait_ge(S["tops_b"], 1)
            own.done(V.tensor_copy(carry[r], Te[0][r, 0:2]))
            own.done(V.tensor_tensor(begun[r], begun[r], carry[r].unsqueeze(2).to_broadcast([HR, 2, P]), ALU.max))
            V.scalar_tensor_tensor(count[r], s_no[r], 1.0, begun[r], ALU.add, ALU.subtract).then_inc(S["tops_in"], 1)
            dve.wait_ge(S["metaT"], 1)
            V.tensor_copy(aim_all[:, :], Td[0][:, 0:TILES]).then_inc(S["meta"], 1)
            V.reciprocal(rc_all[:, :], Td[1][:, 0:TILES]).then_inc(S["meta"], 1)

            def scan(e, i, par, L):
                marks = mask[:, bass.ds(e, 1), :].rearrange("p e i -> p (e i)")
                for h in range(2):
                    dve.wait_ge(S["e1_T" if L == "e1" else "e2_relu"], 2 * e + h + 1)
                    rows_T = Te[h][:, :] if L == "e1" else ehT[:, par, h * HC:(h + 1) * HC]
                    if L == "e1":
                        dve.wait_ge(S["mask_in"][par], 16 * (i + 1))
                    wait(dve, S[L + "_M"], 2 * e + h - 3)
                    wait(dve, S[L + "_scan"], 2 * e + h)
                    before = sums[:, par, HC - 1:HC] if h else sums[:, 1 - par, GROUP - 1:GROUP]
                    if h == 0 and isinstance(e, int) and e == 0:
                        before = 0.0
                    V.tensor_tensor_scan(sums[:, par, h * HC:(h + 1) * HC], marks[:, h * HC:(h + 1) * HC],
                                         rows_T, before, ALU.mult, ALU.add).then_inc(S[L + "_scan"], 1)
                V.tensor_copy(g_idx[:, par, :], src_all[:, bass.ds(K * e + 2 * K, K)]).then_inc(S["next"], 1)

            def over_count(e, h, to, L):
                dve.wait_ge(S[L + "_M"], 2 * e + h + 1)
                rc = rc_all[:, bass.ds(K * e + HT * h, HT)].unsqueeze(2).to_broadcast([P, HT, C])
                V.tensor_tensor(to, Me[h][:, :].rearrange("p (k c) -> p k c", c=C), rc,
                                ALU.mult).then_inc(S[L + "_evac"], 1)

            def edges1(i):
                for par in range(2):
                    e = 2 * i + par
                    if not isinstance(e, int) or e > 0:
                        measure(e, i, par)
                        scales(e, par)
                    scan(e, i, par, "e1")
                    wait(dve, S["e1_add"][par], 16 * K * i)
                    V.tensor_copy(s_idx[:, par, :], aim_all[:, bass.ds(K * e, K)])
                    for h in range(2):
                        over_count(e, h, msg[:, par, HT * h:HT * h + HT, :], "e1")

            edges1(0)
            with dve.Fori(1, EG // 2 - 1) as i:
                own.enter(i - 1, 4)
                edges1(i)
            own.leave(EG // 2 - 2)
            edges1(EG // 2 - 1)

            def residual(j, x_in, par):
                wait(dve, S["d2_stored"][par], 16 * j)
                own.done(V.tensor_tensor(do[:, par, :, :], x_in,
                                         b2b[:, :].unsqueeze(1).to_broadcast([P, K, C]), ALU.add))

            def back2(g, par):
                for h in range(2):
                    dve.wait_ge(S["d2_M"], 2 * g + h + 1)
                    o = flat(do, par)[:, h * HC:(h + 1) * HC]
                    V.tensor_tensor(o, Md[h][:, :], o, ALU.add).then_inc(S["d2_evac"], 1)

            def edge_out(e):
                for h in range(2):
                    over_count(e, h, msg2[:, bass.ds(K * e + HT * h, HT), :], "e2")

            def step2(j, i, epar):
                dve.wait_ge(S["d2_x"][1 - epar], 16 * (i + 1 + epar))
                residual(j + 1, x_even[1 - epar], 0)
                scan(j, i, epar, "e2")
                back2(2 * j + 2, 0)
                residual(j + 1, kept(j + 1), 1)
                edge_out(j)
                back2(2 * j + 3, 1)

            def stage(e, i, par):
                wait(dve, S["e2_add"][par], 16 * K * i)
                V.tensor_copy(s_idx[:, par, :], aim_all[:, bass.ds(e * K, K)])
                V.tensor_copy(msg[:, par, :, :], msg2[:, bass.ds(e * K, K), :]).then_inc(S["staged"], 1)

            dve.wait_ge(S["x_kept"], 16 * (NG // 2 + 1))
            dve.wait_ge(S["d2_x"][0], 16)
            for par, x_in in enumerate((x_even[0], kept(0))):
                residual(0, x_in, par)
                back2(par, par)
            step2(0, 0, 0)
            step2(1, 0, 1)
            dve.wait_ge(S["p1_done"], 1)
            dve.wait_ge(S["e2_evac"], 4)
            stage(0, 0, 0)
            with dve.Fori(1, (EG - 4) // 2) as i:
                own.enter(i - 1, 4)
                step2(2 * i, i, 0)
                step2(2 * i + 1, i, 1)
            own.leave((EG - 4) // 2 - 1)
            step2(EG - 4, EG // 2 - 2, 0)
            residual(NG // 2, kept(EG - 1), 0)
            scan(EG - 3, EG // 2 - 2, 1, "e2")
            back2(NG - 1, 0)
            stage(1, 0, 1)
            edge_out(EG - 3)
            scan(EG - 2, EG // 2 - 1, 0, "e2")
            edge_out(EG - 2)
            scan(EG - 1, EG // 2 - 1, 1, "e2")
            stage(2, 1, 0)
            edge_out(EG - 1)
            dve.wait_ge(S["e2_evac"], 2 * EG)
            stage(3, 1, 1)
            with dve.Fori(2, EG // 2) as i:
                for par in range(2):
                    stage(2 * i + par, i, par)

        @block.scalar
        def _(act):
            A = nc.scalar

            def deviations(g, par):
                act.wait_ge(S["d1_mean"], g + 1)
                wait(act, S["d1_relu"], 2 * g - 2)
                A.activation(d_neg[:, par, :], d_mv[:, par, :, 0], ACT.Copy, scale=-1.0).then_inc(S["d1_neg"], 1)
                A.activation(d_sd[:, par, :], d_mv[:, par, :, 1], ACT.Sqrt, bias=eps[:, :]).then_inc(S["d1_std"], 1)
                wait(act, S["d1_T"], 2 * g - 2)
                act.wait_ge(S["d1_neg"], g + 1)

            def centred(g, par, q, h):
                for k in range(HT * h, HT * h + HT):
                    ins = A.activation(dh[:, par, k, :], x_ring[q][:, k, :], ACT.Relu, bias=d_neg[:, par, k:k + 1])
                ins.then_inc(S["d1_relu"], 1)

            def back(L, g, par):
                for h in range(2):
                    act.wait_ge(S[L + "_T"], 2 * g + h + 1)
                    wait(act, S[L + "_M"], 2 * g + h - 3)
                    to = dT[:, par, h * HC:(h + 1) * HC]
                    if L == "d1":
                        ins = A.activation(to, Td[h][:, :], ACT.Copy)
                    else:
                        ins = A.activation(to, Td[h][:, :], ACT.Relu, bias=b1c[:, :])
                    ins.then_inc(S[L + "_hT"], 1)

            def quad1(i):
                for q in range(4):
                    g, par, q1 = 4 * i + q, q % 2, (q + 1) % 4
                    deviations(g + 1, 1 - par)
                    centred(g + 1, 1 - par, q1, 0)
                    back("d1", g, par)
                    centred(g + 1, 1 - par, q1, 1)

            deviations(0, 0)
            centred(0, 0, 0, 0)
            centred(0, 0, 0, 1)
            quad1(0)
            with act.Fori(1, NG // 4) as i:
                quad1(i)
            back("d1", NG - 1, 0)

            def edges1(i):
                for par in range(2):
                    e = 2 * i + par
                    act.wait_ge(S["e1_mean"], e + 1)
                    A.activation(e_sd[:, par, :], e_mv[:, par, :, 1], ACT.Sqrt, bias=eps[:, :]).then_inc(S["e1_std"], 1)
                    act.wait_ge(S["e1_par"], e + 1)
                    wait(act, S["e1_T"], 2 * e - 2)
                    for h in range(2):
                        for k in range(HT * h, HT * h + HT):
                            ins = A.activation(eh[:, par, k, :], eg[:, par, k, :], ACT.Relu,
                                               bias=e_neg[:, par, k:k + 1], scale=e_rs[:, par, k:k + 1])
                        ins.then_inc(S["e1_relu"], 1)

            edges1(0)
            with act.Fori(1, EG // 2) as i:
                edges1(i)

            def edge2(e, par):
                for h in range(2):
                    act.wait_ge(S["e2_T"], 2 * e + h + 1)
                    wait(act, S["e2_scan"], 2 * e + h - 3)
                    A.activation(ehT[:, par, h * HC:(h + 1) * HC], Te[h][:, :], ACT.Relu,
                                 bias=b1c[:, :]).then_inc(S["e2_relu"], 1)

            def step2(j, epar):
                edge2(j, epar)
                back("d2", 2 * j + 3, 1)
                back("d2", 2 * j + 4, 0)

            act.wait_ge(S["d1_M"], 2 * NG)
            act.wait_ge(S["e1_T"], 2 * EG)
            for g in range(3):
                back("d2", g, g % 2)
            step2(0, 0)
            step2(1, 1)
            with act.Fori(1, (EG - 4) // 2) as i:
                step2(2 * i, 0)
                step2(2 * i + 1, 1)
            step2(EG - 4, 0)
            edge2(EG - 3, 1)
            edge2(EG - 2, 0)
            edge2(EG - 1, 1)

        @block.tensor
        def _(pe):
            T = nc.tensor

            def turn(t, par, h, bank):
                for k in range(HT):
                    ins = T.transpose(bank[:, k * P:(k + 1) * P], t[:, par, HT * h + k, :], ident[:, :])
                return ins

            def dense_T(L, g, par, i):
                for h in range(2):
                    if L == "d1":
                        pe.wait_ge(S["d1_relu"], 2 * g + h + 1)
                    else:
                        pe.wait_ge(S["d2_p"][par], 16 * (i + 1))
                    wait(pe, S[L + "_hT"], 2 * g + h - 1)
                    turn(dh, par, h, Td[h]).then_inc(S[L + "_T"], 1)

            def dense_M(L, g, par, root):
                for h in range(2):
                    pe.wait_ge(S[L + "_hT"], 2 * g + h + 1)
                    wait(pe, S[L + "_evac"], 2 * g + h - 1)
                    for k in range(HT):
                        ins = T.matmul(Md[h][:, k * C:(k + 1) * C], dT[:, par, (HT * h + k) * P:(HT * h + k + 1) * P],
                                       root[:, :], start=True, stop=True)
                    ins.then_inc(S[L + "_M"], 1)

            def edge_T(L, e, par, i):
                for h in range(2):
                    if L == "e1":
                        pe.wait_ge(S["e1_relu"], 2 * e + h + 1)
                        wait(pe, S["e1_scan"], 2 * e + h - 1)
                        turn(eh, par, h, Te[h]).then_inc(S["e1_T"], 1)
                    else:
                        if isinstance(e, int) and e == EG - 1:
                            pe.wait_ge(S["last_in"], 2)
                        else:
                            pe.wait_ge(S["e2_in"][par], 16 * K * (i + 1))
                        wait(pe, S["e2_relu"], 2 * e + h - 1)
                        turn(eg, par, h, Te[h]).then_inc(S["e2_T"], 1)

            def edge_rels(e):
                return [pe.value_load(rels[0:1, bass.ds(2 * e + h, 1)], min_val=0, max_val=16 ** HT - 1)
                        for h in range(2)]

            def edge_M(L, e, par, w, rel):
                for h in range(2):
                    pe.wait_ge(S[L + "_scan"], 2 * e + h + 1)
                    wait(pe, S[L + "_evac"], 2 * e + h - 1)
                    for k in range(HT):
                        col = ((rel[h] >> (4 * k)) & 15) * C + w
                        ins = T.matmul(Me[h][:, k * C:(k + 1) * C], sums[:, par, (HT * h + k) * P:(HT * h + k + 1) * P],
                                       w_all[:, bass.ds(col, C)], start=True, stop=True)
                    ins.then_inc(S[L + "_M"], 1)

            pe.wait_ge(S["made"], 1)
            pe.wait_ge(S["rec_ready"], 1)
            T.matmul(Me[0][:, 0:R], tri, n_f, start=True, stop=True)
            T.matmul(Me[0][:, R:2 * R], ones, n_f, start=True, stop=True).then_inc(S["offs"], 1)

            pe.wait_ge(S["consts_in"], 96)

            def pair1(i):
                dense_M("d1", 2 * i, 0, r1)
                dense_T("d1", 2 * i + 1, 1, i)
                dense_M("d1", 2 * i + 1, 1, r1)
                dense_T("d1", 2 * i + 2, 0, i)

            dense_T("d1", 0, 0, 0)
            pair1(0)
            with pe.Fori(1, NG // 2) as i:
                pair1(i)
            dense_M("d1", NG - 1, 0, r1)

            pe.wait_ge(S["cur_in"], 32)
            for h in range(2):
                ins = T.transpose(Me[1][:, h * HR:(h + 1) * HR], cur[0:HR, h, :, 0], ident[0:HR, 0:HR])
            ins.then_inc(S["src_T"], 1)
            pe.wait_ge(S["d1_hT"], 2 * NG)
            pe.wait_ge(S["tops_in"], 1)
            for h in range(2):
                T.transpose(Td[0][0:1, h * HR:(h + 1) * HR], begun[0:HR, h, P - 1:P], ident[0:HR, 0:HR])
            for h in range(2):
                T.transpose(Td[1][0:1, h * HR:(h + 1) * HR], rel_rf[0:HR, h:h + 1], ident[0:HR, 0:HR])
            ins = T.transpose(Td[1][0:1, TILES:TILES + EG], meet[0:EG], ident[0:EG, 0:EG])
            ins.then_inc(S["tops_t"], 1)
            pe.wait_ge(S["tops_in"], 2)
            for h in range(2):
                ins = T.transpose(Te[0][0:HR, h:h + 1], top_sum[0:1, h * HR:(h + 1) * HR], ident[0:1, 0:1])
            ins.then_inc(S["tops_b"], 1)
            pe.wait_ge(S["tops_in"], 3)
            for h in range(2):
                for bank, a in ((Td[0], aim[0:HR, h, :]), (Td[1], count[0:HR, h, :])):
                    ins = T.transpose(bank[:, h * HR:(h + 1) * HR], a, ident[0:HR, 0:HR])
            ins.then_inc(S["metaT"], 1)

            def edges1(i):
                for par in range(2):
                    rel = edge_rels(2 * i + par)
                    edge_T("e1", 2 * i + par, par, i)
                    edge_M("e1", 2 * i + par, par, 0, rel)

            edges1(0)
            with pe.Fori(1, EG // 2) as i:
                edges1(i)

            def step2(j, i, epar):
                rel = edge_rels(j)
                edge_T("e2", j, epar, i)
                dense_M("d2", 2 * j + 2, 0, r2)
                dense_T("d2", 2 * j + 3, 1, j + 1)
                edge_M("e2", j, epar, R * C, rel)
                dense_M("d2", 2 * j + 3, 1, r2)
                dense_T("d2", 2 * j + 4, 0, j + 2)

            dense_T("d2", 0, 0, 0)
            for g in range(2):
                dense_M("d2", g, g, r2)
                dense_T("d2", g + 1, 1 - g, g)
            step2(0, 0, 0)
            step2(1, 0, 1)
            with pe.Fori(1, (EG - 4) // 2) as i:
                step2(2 * i, i, 0)
                step2(2 * i + 1, i, 1)
            step2(EG - 4, EG // 2 - 2, 0)
            for e in range(EG - 3, EG):
                rel = edge_rels(e)
                edge_T("e2", e, e % 2, e // 2)
                if e == EG - 3:
                    dense_M("d2", NG - 1, 0, r2)
                edge_M("e2", e, e % 2, R * C, rel)


_NAMES = {"x": "x", "src": "src", "dst": "dst", "attr": "edge_attr_42",
          "w_rel1": "L0_gnn_w_rel1", "root1": "L0_gnn_root1", "b1": "L0_gnn_b1",
          "w_rel2": "L0_gnn_w_rel2", "root2": "L0_gnn_root2", "b2": "L0_gnn_b2"}


def kernel(**inputs):
    import numpy as np
    import concourse.bacc as bacc
    from concourse.bass_utils import run_bass_kernel_spmd

    nc = bacc.Bacc("TRN2", target_bir_lowering=False, num_devices=1)
    arrays, args = {}, []
    for short, name in _NAMES.items():
        a = np.ascontiguousarray(inputs[name])
        if short in ("src", "dst"):
            a = a.reshape(-1, 1)
        arrays[f"in_{short}"] = a
        args.append(nc.dram_tensor(f"in_{short}", a.shape, mybir.dt.from_np(a.dtype), kind="ExternalInput").ap())
    args.append(nc.dram_tensor("out_rows", (N + SPARE, C), F32, kind="ExternalOutput").ap())
    build(nc, *args)
    r = run_bass_kernel_spmd(nc, [arrays], core_ids=[0])
    return r.results[0]["out_rows"][:N]
```
